# Optimizing a Trainium2 kernel written in Bass

```python
import numpy as np
import jax
import jax.numpy as jnp

def _softmax(x, axis=-1):
    return jax.nn.softmax(x, axis=axis)

def _gelu(x):
    return jax.nn.gelu(x, approximate=True)

def _silu(x):
    return jax.nn.silu(x)

def _sigmoid(x):
    return jax.nn.sigmoid(x)

def _layernorm(x, axis=-1, eps=1e-05):
    m = jnp.mean(x, axis=axis, keepdims=True)
    v = jnp.var(x, axis=axis, keepdims=True)
    return (x - m) / jnp.sqrt(v + eps)

def _scatter_add(tgt, idx, src, axis=0):
    return tgt.at[idx].add(src)

def _segment_sum(src, seg, n):
    return jax.ops.segment_sum(src, seg, n)
kernel_name = 'mk_cond_resid_d4_seqx_r4_8253bb'

def setup_inputs(seed: int=0):
    np.random.seed(seed)
    _w = jnp.asarray

    def _rec_inputs():
        import jax
        import jax.numpy as jnp
        _rk = jax.random.key(seed)
        x = -0.000125 + 0.9999 * jax.random.normal(jax.random.fold_in(_rk, 1), (8, 256, 256), jnp.float32)
        _lenS = 256 - jax.random.randint(jax.random.fold_in(_rk, 7), (8,), 0, max(1, 256 // 4) + 1, jnp.int32)
        _lenS2 = 256 - jax.random.randint(jax.random.fold_in(_rk, 8), (8,), 0, max(1, 256 // 4) + 1, jnp.int32)
        cond_1024 = -0.00493535 + 1.00056 * jax.random.normal(jax.random.fold_in(_rk, 11), (8, 256), jnp.float32)
        return (x, cond_1024)
    x, cond_1024 = _rec_inputs()

    def _L0_cond_setup():
        import jax, jax.numpy as jnp
        import numpy as np
        import math
        D = 256
        H = 256
        key = jax.random.key(seed)
        k1, k2, k3, k4 = jax.random.split(key, 4)
        x = jax.random.normal(k1, (64, 128, D), dtype=jnp.float32)
        h0 = jax.random.normal(k2, (64, H), dtype=jnp.float32)
        Wx = jax.random.normal(k3, (D, 4 * H), dtype=jnp.float32) / math.sqrt(D)
        Wh = jax.random.normal(k4, (H, 4 * H), dtype=jnp.float32) / math.sqrt(H)
        b = jnp.zeros((4 * H,), dtype=jnp.float32)
        return {'x': x, 'h0': h0, 'Wx': Wx, 'Wh': Wh, 'b': b}
    _L0_cond_all = _L0_cond_setup()
    _L0_cond_in = {k: v for k, v in _L0_cond_all.items() if k in ('Wx', 'Wh', 'b')}
    del _L0_cond_all

    def _L1_cond_setup():
        import jax, jax.numpy as jnp
        import numpy as np
        N, T, D, H = (128, 128, 256, 256)
        key = jax.random.key(seed)
        k1, k2, k3, k4 = jax.random.split(key, 4)
        x = jax.random.normal(k1, (N, T, D), dtype=jnp.float32)
        h0 = jax.random.normal(k2, (N, H), dtype=jnp.float32)
        Wx = jax.random.normal(k3, (D, H), dtype=jnp.float32) / np.sqrt(D)
        Wh = jax.random.normal(k4, (H, H), dtype=jnp.float32) / np.sqrt(H)
        b = jnp.zeros((H,), dtype=jnp.float32)
        return {'x': x, 'h0': h0, 'Wx': Wx, 'Wh': Wh, 'b': b}
    _L1_cond_all = _L1_cond_setup()
    _L1_cond_in = {k: v for k, v in _L1_cond_all.items() if k in ('Wx', 'Wh', 'b')}
    del _L1_cond_all

    def _L2_cond_setup():
        import jax, jax.numpy as jnp
        import numpy as np
        NUM_EXPERTS = 4
        TOP_K = 2
        key = jax.random.key(seed)
        ks = jax.random.split(key, 16)
        B, L, D, E, H = (8, 192, 256, NUM_EXPERTS, 1024)
        s = 0.02
        return {'context_c': jax.random.normal(ks[0], (B, L, D), jnp.float32), 'time_cond': jax.random.normal(ks[1], (B, D), jnp.float32), 'gate_w': jax.random.normal(ks[2], (3 * D, E), jnp.float32) * s, 'gate_b': jnp.zeros((E,), jnp.float32), 'time_w': jax.random.normal(ks[3], (D, 2 * E), jnp.float32) * s, 'time_b': jnp.zeros((2 * E,), jnp.float32), 'ew1': jax.random.normal(ks[4], (E, D, H), jnp.float32) * s, 'eb1': jnp.zeros((E, H), jnp.float32), 'ew2': jax.random.normal(ks[5], (E, H, D), jnp.float32) * s, 'eb2': jnp.zeros((E, D), jnp.float32), 'sw1': jax.random.normal(ks[6], (D, H), jnp.float32) * s, 'sb1': jnp.zeros((H,), jnp.float32), 'sw2': jax.random.normal(ks[7], (H, D), jnp.float32) * s, 'sb2': jnp.zeros((D,), jnp.float32)}
    _L2_cond_all = _L2_cond_setup()
    _L2_cond_in = {k: v for k, v in _L2_cond_all.items() if k in ('gate_w', 'gate_b', 'time_w', 'time_b', 'ew1', 'eb1', 'ew2', 'eb2', 'sw1', 'sb1', 'sw2', 'sb2')}
    del _L2_cond_all

    def _L3_cond_setup():
        import jax, jax.numpy as jnp
        import numpy as np
        import math
        N, T, D, H = (64, 128, 256, 256)
        key = jax.random.key(seed)
        k1, k2, k3, k4 = jax.random.split(key, 4)
        x = jax.random.normal(k1, (N, T, D), dtype=jnp.float32)
        h0 = jax.random.normal(k2, (N, H), dtype=jnp.float32)
        Wx = jax.random.normal(k3, (D, 4 * H), dtype=jnp.float32) / math.sqrt(D)
        Wh = jax.random.normal(k4, (H, 4 * H), dtype=jnp.float32) / math.sqrt(H)
        b = jnp.zeros((4 * H,), dtype=jnp.float32)
        return {'x': x, 'h0': h0, 'Wx': Wx, 'Wh': Wh, 'b': b}
    _L3_cond_all = _L3_cond_setup()
    _L3_cond_in = {k: v for k, v in _L3_cond_all.items() if k in ('Wx', 'Wh', 'b')}
    del _L3_cond_all
    return {'x': x, 'cond_1024': cond_1024, 'L0_cond_Wx': _L0_cond_in['Wx'], 'L0_cond_Wh': _L0_cond_in['Wh'], 'L0_cond_b': _L0_cond_in['b'], 'L1_cond_Wx': _L1_cond_in['Wx'], 'L1_cond_Wh': _L1_cond_in['Wh'], 'L1_cond_b': _L1_cond_in['b'], 'L2_cond_gate_w': _L2_cond_in['gate_w'], 'L2_cond_gate_b': _L2_cond_in['gate_b'], 'L2_cond_time_w': _L2_cond_in['time_w'], 'L2_cond_time_b': _L2_cond_in['time_b'], 'L2_cond_ew1': _L2_cond_in['ew1'], 'L2_cond_eb1': _L2_cond_in['eb1'], 'L2_cond_ew2': _L2_cond_in['ew2'], 'L2_cond_eb2': _L2_cond_in['eb2'], 'L2_cond_sw1': _L2_cond_in['sw1'], 'L2_cond_sb1': _L2_cond_in['sb1'], 'L2_cond_sw2': _L2_cond_in['sw2'], 'L2_cond_sb2': _L2_cond_in['sb2'], 'L3_cond_Wx': _L3_cond_in['Wx'], 'L3_cond_Wh': _L3_cond_in['Wh'], 'L3_cond_b': _L3_cond_in['b']}

def reference(x, cond_1024, L0_cond_Wx, L0_cond_Wh, L0_cond_b, L1_cond_Wx, L1_cond_Wh, L1_cond_b, L2_cond_gate_w, L2_cond_gate_b, L2_cond_time_w, L2_cond_time_b, L2_cond_ew1, L2_cond_eb1, L2_cond_ew2, L2_cond_eb2, L2_cond_sw1, L2_cond_sb1, L2_cond_sw2, L2_cond_sb2, L3_cond_Wx, L3_cond_Wh, L3_cond_b):
    import jax
    import jax.numpy as jnp

    def _L0_cond_ref(x, h0, Wx, Wh, b):
        import jax, jax.numpy as jnp
        import numpy as np
        import math
        D = 256
        H = 256
        xz = jnp.einsum('ntd,dk->ntk', x, Wx) + b
        c0 = jnp.zeros_like(h0)

        def step(carry, xz_t):
            prev_h, prev_c = carry
            z = xz_t + prev_h @ Wh
            ai, af, ao, ag = jnp.split(z, 4, axis=1)
            i = jax.nn.sigmoid(ai)
            f = jax.nn.sigmoid(af)
            o = jax.nn.sigmoid(ao)
            g = jnp.tanh(ag)
            next_c = f * prev_c + i * g
            next_h = o * jnp.tanh(next_c)
            return ((next_h, next_c), next_h)
        _, hs = jax.lax.scan(step, (h0, c0), jnp.swapaxes(xz, 0, 1))
        return jnp.swapaxes(hs, 0, 1)

    def _L1_cond_ref(x, h0, Wx, Wh, b):
        import jax, jax.numpy as jnp
        import numpy as np
        N, T, D, H = (128, 128, 256, 256)
        xp = jnp.einsum('ntd,dh->nth', x, Wx) + b

        def step(prev_h, xp_t):
            next_h = jnp.tanh(xp_t + prev_h @ Wh)
            return (next_h, next_h)
        _, h = jax.lax.scan(step, h0, jnp.swapaxes(xp, 0, 1))
        return jnp.swapaxes(h, 0, 1)

    def _L2_cond_ref(context_c, time_cond, gate_w, gate_b, time_w, time_b, ew1, eb1, ew2, eb2, sw1, sb1, sw2, sb2):
        import jax, jax.numpy as jnp
        import numpy as np
        NUM_EXPERTS = 4
        TOP_K = 2
        B, L, D = context_c.shape
        E, K = (NUM_EXPERTS, TOP_K)
        L_head = L_wrist = L // 3
        head = context_c[:, :L_head]
        wrist = context_c[:, L_head:L_head + L_wrist]
        proprio = context_c[:, L_head + L_wrist:]
        full_agg = context_c.mean(axis=1)
        hp_agg = jnp.concatenate([head, proprio], axis=1).mean(axis=1)
        wp_agg = jnp.concatenate([wrist, proprio], axis=1).mean(axis=1)
        gate_in = jnp.concatenate([full_agg, hp_agg, wp_agg], axis=-1)
        gate_logits = gate_in @ gate_w + gate_b
        mod = jax.nn.silu(time_cond) @ time_w + time_b
        scale, shift = jnp.split(mod, 2, axis=-1)
        gate_logits = gate_logits * (1.0 + scale) + shift
        gate_scores = jax.nn.softmax(gate_logits, axis=-1)
        topk_w, topk_i = jax.lax.top_k(gate_scores, K)
        topk_w = topk_w / (topk_w.sum(axis=-1, keepdims=True) + 1e-08)
        onehot = (topk_i[..., None] == jnp.arange(E)[None, None, :]).astype(context_c.dtype)
        w_be = jnp.sum(topk_w[..., None] * onehot, axis=1)
        mask = np.ones((E, L), dtype=np.float32)
        mask[1, L_head:L_head + L_wrist] = 0.0
        mask[2, :L_head] = 0.0
        mask = jnp.asarray(mask)
        out = jnp.zeros_like(context_c)
        for e in range(E):
            h = jax.nn.gelu(context_c @ ew1[e] + eb1[e], approximate=True)
            y = h @ ew2[e] + eb2[e]
            out = out + w_be[:, e][:, None, None] * mask[e][None, :, None] * y
        shared = jax.nn.gelu(context_c @ sw1 + sb1, approximate=True) @ sw2 + sb2
        return out + shared

    def _L3_cond_ref(x, h0, Wx, Wh, b):
        import jax, jax.numpy as jnp
        import numpy as np
        import math
        N, T, D, H = (64, 128, 256, 256)
        Hdim = h0.shape[1]
        c0 = jnp.zeros_like(h0)
        xW = jnp.einsum('ntd,dk->tnk', x, Wx) + b

        def step(carry, xw_t):
            prev_h, prev_c = carry
            a = xw_t + prev_h @ Wh
            i = jax.nn.sigmoid(a[:, :Hdim])
            f = jax.nn.sigmoid(a[:, Hdim:2 * Hdim])
            o = jax.nn.sigmoid(a[:, 2 * Hdim:3 * Hdim])
            g = jnp.tanh(a[:, 3 * Hdim:])
            next_c = f * prev_c + i * g
            next_h = o * jnp.tanh(next_c)
            return ((next_h, next_c), next_h)
        _, hs = jax.lax.scan(step, (h0, c0), xW)
        return jnp.transpose(hs, (1, 0, 2))
    x = x + _L0_cond_ref(x, cond_1024, L0_cond_Wx, L0_cond_Wh, L0_cond_b)
    x = x + _L1_cond_ref(x, cond_1024, L1_cond_Wx, L1_cond_Wh, L1_cond_b)
    x = x + _L2_cond_ref(x, cond_1024, L2_cond_gate_w, L2_cond_gate_b, L2_cond_time_w, L2_cond_time_b, L2_cond_ew1, L2_cond_eb1, L2_cond_ew2, L2_cond_eb2, L2_cond_sw1, L2_cond_sb1, L2_cond_sw2, L2_cond_sb2)
    x = x + _L3_cond_ref(x, cond_1024, L3_cond_Wx, L3_cond_Wh, L3_cond_b)
    return x

_drawn_inputs = setup_inputs


def setup_inputs(seed=0):
    import zlib

    import numpy as np

    out = dict(_drawn_inputs(seed))
    spreads = {'L0_cond_b': (0.0, 0.1),
     'L1_cond_b': (0.0, 0.1),
     'L2_cond_gate_b': (0.0, 0.1),
     'L2_cond_time_b': (0.0, 0.1),
     'L2_cond_eb1': (0.0, 0.403),
     'L2_cond_eb2': (0.0, 0.1),
     'L2_cond_sb1': (0.0, 0.267),
     'L2_cond_sb2': (0.0, 0.1),
     'L3_cond_b': (0.0, 0.287)}
    factors = {'L2_cond_gate_w': 2.907}
    for name, (base, spread) in spreads.items():
        noise = np.random.default_rng([zlib.crc32(name.encode()), seed]).standard_normal(out[name].shape)
        drawn = base * np.exp(spread * noise) if base else spread * noise
        out[name] = jnp.asarray(drawn.astype(out[name].dtype))
    for name, factor in factors.items():
        out[name] = (out[name] * factor).astype(out[name].dtype)
    return out
```

```python
from contextlib import ExitStack

import concourse.bass as bass
from concourse import mybir

F32 = mybir.dt.float32
F32R = mybir.dt.float32r
ALU = mybir.AluOpType
ACT = mybir.ActivationFunctionType
AX_X = mybir.AxisListType.X

P = 128
HALVES = 2
GATES = 4
GATE_COLUMN = (3, 0, 1, 2)
BLOCK = 16
PASS = 2 * BLOCK
RNN_LAG = BLOCK
MOE_LAG = BLOCK + RNN_LAG
GROUP = 4
TANH_SCALE = 0.7978845608028654
CUBIC = 0.044715


def cond_residual_kernel(nc, x, cond_1024, L0_Wx, L0_Wh, L0_b, L1_Wx, L1_Wh, L1_b, gate_w, gate_b, time_w, time_b,
                         ew1, eb1, ew2, eb2, sw1, sb1, sw2, sb2, L3_Wx, L3_Wh, L3_b, out):
    B, T, D = x.shape
    E, _, H = ew1.shape
    assert D == HALVES * P and B == 8 and T % PASS == 0 and L0_Wh.shape == (D, GATES * D)
    PASSES = T // PASS
    BLOCKS = T // BLOCK
    TOK = BLOCK * B
    COLS = HALVES * B
    NE = E + 1
    TILES = H // P
    GPE = TILES // GROUP
    GROUPS = NE * GPE
    THIRD = T // 3
    SPANS = ((0, THIRD), (THIRD, 2 * THIRD), (2 * THIRD, T))

    items = []
    for q in range(GROUPS + 2):
        if q < GROUPS:
            items.append(("up", q))
        if q >= 2:
            items.append(("down", q - 2))
    MM_PER_ITEM = GROUP * HALVES
    MM_PER_STEP = len(items) * MM_PER_ITEM // BLOCK
    assert MM_PER_STEP * BLOCK == len(items) * MM_PER_ITEM
    last_step = {it: ((n + 1) * MM_PER_ITEM - 1) // MM_PER_STEP for n, it in enumerate(items)}

    ROWS = {}
    at = 0
    for name, rows in (("eb1", E * TILES), ("sb1", TILES), ("eb2", E * HALVES), ("sb2", HALVES),
                       ("L0_b", GATES * HALVES), ("L1_b", HALVES), ("L3_b", GATES * HALVES), ("cond", B * HALVES)):
        ROWS[name] = at
        at += rows
    NROWS = at

    with ExitStack() as ctx:
        def sb(name, shape, dt=F32):
            return ctx.enter_context(nc.sbuf_tensor(name, shape, dt))

        def psum(name):
            return ctx.enter_context(nc.psum_tensor(name, [P, 512], F32))

        def sem(name):
            return ctx.enter_context(nc.semaphore(name))

        wx = {0: sb("wx0", [P, HALVES, GATES * D]), 3: sb("wx3", [P, HALVES, GATES * D])}
        wh = sb("wh", [P, HALVES, GATES * D])
        wh_hi = sb("wh_hi", [P, HALVES, GATES * D], F32R)
        wh_lo = sb("wh_lo", [P, HALVES, GATES * D], F32R)
        wx1 = sb("wx1", [P, HALVES, D])
        wh1 = sb("wh1", [P, HALVES, D])
        up_w = sb("up_w", [P, NE, HALVES, H])
        down_w = sb("down_w", [P, NE, TILES, D])
        rows = sb("rows", [P, P])
        vec = sb("vec", [P, P])
        gate_w_sb = sb("gate_w_sb", [P, 3 * HALVES, E])
        time_w_sb = sb("time_w_sb", [P, HALVES, 2 * E])
        gate_b_sb = sb("gate_b_sb", [1, E])
        time_b_sb = sb("time_b_sb", [1, 2 * E])
        ident = sb("ident", [P, P])
        ones = sb("ones", [P, P])
        keep = sb("keep", [P, 2, T])
        x_rows = sb("x_rows", [P, D])
        xT = sb("xT", [P, 2, BLOCK, HALVES, B])
        xz = sb("xz", [P, 2, BLOCK, HALVES, GATES, B])
        h_seq = sb("h_seq", [P, BLOCK, HALVES, B])
        h_hi = sb("h_hi", [P, 2, HALVES, B], F32R)
        h_lo = sb("h_lo", [P, 2, HALVES, B], F32R)
        sig = sb("sig", [P, HALVES, 3 * B])
        gc = sb("gc", [P, HALVES, 2 * B])
        prod = sb("prod", [P, HALVES, 2 * B])
        tanh_c = sb("tanh_c", [P, HALVES, B])
        rnn_x = sb("rnn_x", [P, 2, BLOCK, HALVES, B])
        rnn_xz = sb("rnn_xz", [P, 2, BLOCK, HALVES, B])
        rnn_h = sb("rnn_h", [P, 2, BLOCK, HALVES, B])
        x1 = sb("x1", [P, 2, BLOCK, HALVES, B])
        x1_all = sb("x1_all", [P, T, HALVES, B])
        u = sb("u", [P, 4, GROUP * TOK])
        inner = sb("inner", [P, 2, GROUP * TOK])
        hid = sb("hid", [P, 4, GROUP * TOK])
        y = sb("y", [P, NE, BLOCK, HALVES, B])
        sums = sb("sums", [P, 3, HALVES, B])
        gate_in = sb("gate_in", [P, 3, HALVES, B])
        gtmp = sb("gtmp", [P, COLS])
        silu = sb("silu", [P, COLS])
        gs = sb("gs", [B, 80])
        spread = sb("spread", [B, E, B])
        wb = sb("wb", [P, E, B])
        y_back = y
        x2 = sb("x2", [P, 2, BLOCK, HALVES, B])
        part = sb("part", [P, BLOCK, HALVES, B])
        x3 = sb("x3", [P, HALVES, B, BLOCK])
        out_rows = sb("out_rows", [P, D])

        z = [psum("z_half0"), psum("z_half1")]
        z1 = psum("z_rnn")
        up_ps = [psum("up0"), psum("up1")]
        down_ps = psum("down")
        bulk = [psum("bulk0"), psum("bulk1")]

        y_dram = nc.dram_tensor("expert_out", [BLOCKS, NE, P, BLOCK * COLS], F32, kind="Internal").ap()

        rows_in = sem("rows_in")
        x_in = sem("x_in")
        wx0_in, wh0_in, w1_in, moe_in, gate_in_sem, wx3_in, wh3_in = (
            sem(n) for n in ("wx0_in", "wh0_in", "w1_in", "moe_in", "gate_params_in", "wx3_in", "wh3_in"))
        consts = sem("consts")
        vec_ps, vec_ready = sem("vec_ps"), sem("vec_ready")
        wh_split = sem("wh_split")
        wh_step = sem("wh_step")
        xT_ps, xT_ready = sem("xT_ps"), sem("xT_ready")
        xz_ps, xz_ready = sem("xz_ps"), sem("xz_ready")
        def pair(name):
            return [sem(name + "0"), sem(name + "1")]
        z_ready = pair("z_ready")
        gates_ready = pair("gates_ready")
        prod_ready = pair("prod_ready")
        cell_ready = pair("cell_ready")
        cell_tanh = pair("cell_tanh")
        hi_ready, full_ready, lo_ready = pair("hi_ready"), pair("full_ready"), pair("lo_ready")
        rnn_x_ready, rnn_xz_ps, rnn_xz_ready = sem("rnn_x_ready"), sem("rnn_xz_ps"), sem("rnn_xz_ready")
        rnn_z, rnn_h_ready = sem("rnn_z"), sem("rnn_h_ready")
        x1_ready, x1_kept = sem("x1_ready"), sem("x1_kept")
        up_done, u_ready, poly_done, th_done, hid_ready = (
            sem(n) for n in ("up_done", "u_ready", "poly_done", "th_done", "hid_ready"))
        pool_chain, sq_ready = sem("pool_chain"), sem("sq_ready")
        down_done, y_evac, y_masked = sem("down_done"), sem("y_evac"), sem("y_masked")
        y_shared = sem("y_shared")
        pool_c = sem("pool_consts")
        y_stored = [sem(f"y_stored{e}") for e in range(NE)]
        g_dve, g_act, g_pe = sem("gate_dve"), sem("gate_act"), sem("gate_pe")
        wb_ready = sem("wb_ready")
        y_loaded, x2_chain, x2_ready = sem("y_loaded"), sem("x2_chain"), sem("x2_ready")
        x3_ready, out_ps, out_ready, stored = sem("x3_ready"), sem("out_ps"), sem("out_ready"), sem("stored")
        g_chain, g_shifted = sem("gate_chain"), sem("gate_shifted")

        block = ctx.enter_context(nc.Block())

        def column(name, n=0):
            return vec[:, ROWS[name] + n:ROWS[name] + n + 1]

        def columns(name, n, start=0):
            return vec[:, ROWS[name] + start:ROWS[name] + start + n]

        def bias_over(name, n, start):
            return columns(name, n, start)[:, :, None].to_broadcast([P, n, TOK])

        def passes(eng, body, between=lambda: None):
            body(0, True)
            between()
            with eng.Fori(1, PASSES) as i:
                body(i, False)
            body(PASSES, False)

        def passed(i, s, lag):
            return not isinstance(i, int) or PASS * i + s >= lag


        def lstm_on(i):
            return not (isinstance(i, int) and i == PASSES)

        def rnn_at(i, s):
            if not passed(i, s, RNN_LAG):
                return None
            if isinstance(i, int) and PASS * i + s - RNN_LAG >= T:
                return None
            t = s - RNN_LAG
            return t % BLOCK, (t // BLOCK) % 2, i * PASS + t, 2 * i + t // BLOCK

        def moe_at(i, s):
            if not passed(i, s, MOE_LAG):
                return None
            w = s - MOE_LAG
            return w % BLOCK, 2 * i + w // BLOCK, (w // BLOCK) % 2

        @block.sync
        def _(sp):
            sp.dma_start(x_rows[:], x[:, 0:BLOCK, :]).then_inc(x_in, 16)
            n = 0
            for name, src in (("eb1", eb1.rearrange("e (j p) -> (e j) p", p=P)),
                              ("sb1", sb1.rearrange("(j p) -> j p", p=P)),
                              ("eb2", eb2.rearrange("e (j p) -> (e j) p", p=P)),
                              ("sb2", sb2.rearrange("(j p) -> j p", p=P)),
                              ("L0_b", L0_b.rearrange("(j p) -> j p", p=P)),
                              ("L1_b", L1_b.rearrange("(j p) -> j p", p=P)),
                              ("L3_b", L3_b.rearrange("(j p) -> j p", p=P)),
                              ("cond", cond_1024.rearrange("b (j p) -> (b j) p", p=P))):
                sp.dma_start(rows[ROWS[name]:ROWS[name] + src.shape[0], :], src).then_inc(rows_in, 16)
            sp.dma_start(wx[0][:], L0_Wx.rearrange("(k p) n -> p k n", p=P)).then_inc(wx0_in, 16)
            sp.dma_start(wh[:], L0_Wh.rearrange("(k p) n -> p k n", p=P)).then_inc(wh0_in, 16)
            sp.dma_start(wx1[:], L1_Wx.rearrange("(k p) n -> p k n", p=P)).then_inc(w1_in, 16)
            sp.dma_start(wh1[:], L1_Wh.rearrange("(k p) n -> p k n", p=P)).then_inc(w1_in, 16)
            for e in range(NE):
                w1 = ew1[e] if e < E else sw1
                w2 = ew2[e] if e < E else sw2
                sp.dma_start(up_w[:, e], w1.rearrange("(k p) n -> p k n", p=P)).then_inc(moe_in, 16)
                sp.dma_start(down_w[:, e], w2.rearrange("(j p) n -> p j n", p=P)).then_inc(moe_in, 16)
            sp.dma_start(gate_w_sb[:], gate_w.rearrange("(k p) n -> p k n", p=P)).then_inc(gate_in_sem, 16)
            sp.dma_start(time_w_sb[:], time_w.rearrange("(k p) n -> p k n", p=P)).then_inc(gate_in_sem, 16)
            sp.dma_start(gate_b_sb[:], gate_b.rearrange("(a n) -> a n", a=1)).then_inc(gate_in_sem, 16)
            sp.dma_start(time_b_sb[:], time_b.rearrange("(a n) -> a n", a=1)).then_inc(gate_in_sem, 16)
            sp.dma_start(wx[3][:], L3_Wx.rearrange("(k p) n -> p k n", p=P)).then_inc(wx3_in, 16)

            sp.wait_ge(wh_split, 1)
            sp.dma_start(wh[:], L3_Wh.rearrange("(k p) n -> p k n", p=P)).then_inc(wh3_in, 16)

            def body(i, first):
                for s in range(PASS):
                    if lstm_on(i) and s in (0, BLOCK):
                        load_x(2 * i + s // BLOCK + 1)
                    moe = moe_at(i, s)
                    if moe is not None:
                        w, c, parity = moe
                        for e in range(NE):
                            if w == last_step[("down", GPE * (e + 1) - 1)]:
                                if e == E:
                                    sp.wait_ge(y_shared, c + 2)
                                elif e in (1, 2):
                                    sp.wait_ge(y_masked, 2 * c + e)
                                else:
                                    sp.wait_ge(y_evac, 2 * (NE * c + e + 1))
                                sp.dma_start(y_dram[c, e] if isinstance(c, int) else
                                             y_dram[bass.ds(c, 1), e].rearrange("a p n -> (a p) n"),
                                             y[:, e].rearrange("p t h b -> p (t h b)")).then_inc(y_stored[e], 16)

            def load_x(n):
                sp.wait_ge(xT_ps, n)
                sp.dma_start(x_rows[:], x[:, bass.ds(n % BLOCKS * BLOCK, BLOCK), :]).then_inc(x_in, 16)

            passes(sp, body)

            def load_y(n):
                for e in range(NE):
                    sp.dma_start(y_back[:, e].rearrange("p t h b -> p (t h b)"),
                                 y_dram[n, e] if isinstance(n, int) else
                                 y_dram[bass.ds(n, 1), e].rearrange("a p n -> (a p) n")).then_inc(y_loaded, 16)

            for e in range(NE):
                sp.wait_ge(y_stored[e], 16 * BLOCKS)
            load_y(0)

            def body_b(i, last):
                for s in range(PASS):
                    if s in (0, BLOCK) and not (last and s == BLOCK):
                        n = 2 * i + s // BLOCK + 1
                        sp.wait_ge(x2_ready, n)
                        load_y(n)
                    if s % BLOCK == 4 and (s > BLOCK or not (isinstance(i, int) and i == 0)):
                        store(2 * i + s // BLOCK - 1)

            def store(n):
                sp.wait_ge(out_ready, n + 1)
                sp.dma_start(out[:, bass.ds(n * BLOCK, BLOCK), :], out_rows[:]).then_inc(stored, 16)

            body_b(0, False)
            with sp.Fori(1, PASSES - 1) as i:
                body_b(i, False)
            body_b(PASSES - 1, True)
            store(BLOCKS - 1)
            sp.wait_ge(stored, 16 * BLOCKS)

        @block.tensor
        def _(pe):
            def mm(out_ap, lhsT, rhs, start, stop):
                return nc.tensor.matmul(out_ap, lhsT, rhs, start=start, stop=stop, skip_group_check=True)

            def weight(w, k, gate, m):
                c = GATE_COLUMN[gate] * D + m * P
                return w[:, k, c:c + P]

            def transposes(n):
                pe.wait_ge(x_in, 16 * (n + 1))
                if not (isinstance(n, int) and n == 0):
                    pe.wait_ge(xz_ready, 2 * n)
                for k in range(HALVES):
                    last = nc.tensor.transpose(bulk[0][:, k * TOK:(k + 1) * TOK], x_rows[:, k * P:(k + 1) * P], ident[:])
                last.then_inc(xT_ps, 1)

            def x_products(w, rhs, half, gate, k):
                return mm(bulk[half][:, gate * TOK:(gate + 1) * TOK].rearrange("p (t b) -> p t b", b=B),
                          weight(w, k, gate, half), rhs[:, :, k, :], k == 0, k == HALVES - 1)

            def lstm_step(step, starts, slot_parity, xz_slot, first):
                for m in range(HALVES):
                    if not first:
                        pe.wait_ge(gates_ready[m], 2 * step)
                    mm(z[m][:, 0:GATES * B], ident[:], xz_slot[:, m].rearrange("p g b -> p (g b)"), True, False)
                prev = 1 - slot_parity
                for k in range(HALVES):
                    pe.wait_ge(hi_ready[k], step + starts)
                    for part_ in ("hi", "lo"):
                        if part_ == "lo":
                            if k == 0:
                                pe.wait_ge(lo_ready[k], step + starts)
                        if k == 0:
                            for m in range(HALVES):
                                for gate in range(GATES):
                                    o = z[m][:, gate * B:(gate + 1) * B]
                                    if part_ == "hi":
                                        mm(o, weight(wh_hi, k, gate, m), h_hi[:, prev, k], False, False)
                                        mm(o, weight(wh_lo, k, gate, m), h_hi[:, prev, k], False, False)
                                    else:
                                        mm(o, weight(wh_hi, k, gate, m), h_lo[:, prev, k], False, False)
                    if k == 1:
                        for m in range(HALVES):
                            for gate in range(GATES):
                                o = z[m][:, gate * B:(gate + 1) * B]
                                mm(o, weight(wh_lo, k, gate, m), h_hi[:, prev, k], False, False)
                                mm(o, weight(wh_hi, k, gate, m), h_hi[:, prev, k], False, False)
                                if m == 0 and gate == 0:
                                    pe.wait_ge(lo_ready[k], step + starts)
                                last = mm(o, weight(wh_hi, k, gate, m), h_lo[:, prev, k], False, True)
                            last.then_inc(z_ready[m], 1)

            def rnn_step(slot, parity, done, c):
                if slot == 0:
                    pe.wait_ge(rnn_x_ready, c + 1)
                    if not (isinstance(c, int) and c == 0):
                        pe.wait_ge(rnn_h_ready, done + 1)
                    for m in range(HALVES):
                        for k in range(HALVES):
                            last = mm(z1[:, COLS + m * TOK:COLS + (m + 1) * TOK].rearrange("p (t b) -> p t b", b=B),
                                      wx1[:, k, m * P:(m + 1) * P], rnn_x[:, parity, :, k, :], k == 0, k == 1)
                    last.then_inc(rnn_xz_ps, 1)
                    pe.wait_ge(rnn_xz_ready, c + 1)
                pe.wait_ge(rnn_h_ready, done + 1)
                before = rnn_h[:, (parity if slot else 1 - parity), (slot - 1) % BLOCK]
                mm(z1[:, 0:COLS], ident[:], rnn_xz[:, parity, slot].rearrange("p h b -> p (h b)"), True, False)
                for k in range(HALVES):
                    for m in range(HALVES):
                        last = mm(z1[:, m * B:(m + 1) * B], wh1[:, k, m * P:(m + 1) * P], before[:, k], False, k == 1)
                last.then_inc(rnn_z, 1)

            def moe_products(w, c, parity):
                for n in range(w * MM_PER_STEP, (w + 1) * MM_PER_STEP):
                    kind, q = items[n // MM_PER_ITEM]
                    r = n % MM_PER_ITEM
                    e, g = q // GPE, q % GPE
                    if kind == "up":
                        if r == 0:
                            if q == 0:
                                pe.wait_ge(x1_ready, c + 1)
                            if q >= 1:
                                pe.wait_ge(u_ready, GROUPS * c + q - 1)
                        j, k = r // HALVES, r % HALVES
                        last = mm(up_ps[q % 2][:, j * TOK:(j + 1) * TOK].rearrange("p (t b) -> p t b", b=B),
                                  up_w[:, e, k, (GROUP * g + j) * P:(GROUP * g + j + 1) * P],
                                  x1[:, parity, :, k, :], k == 0, k == 1)
                        if r == MM_PER_ITEM - 1:
                            last.then_inc(up_done, 1)
                    else:
                        yp = down_ps
                        if r == 0:
                            pe.wait_ge(hid_ready, GROUPS * c + q + 1)
                            if g == 0 and not (isinstance(c, int) and c == 0 and e == 0):
                                pe.wait_ge(y_evac, 2 * (NE * c + e))
                        m, j = r // GROUP, r % GROUP
                        last = mm(yp[:, m * TOK:(m + 1) * TOK],
                                  down_w[:, e, GROUP * g + j, m * P:(m + 1) * P],
                                  hid[:, q % 4, j * TOK:(j + 1) * TOK], g == 0 and r == 0, g == GPE - 1 and j == GROUP - 1)
                        if r == MM_PER_ITEM - 1 and g == GPE - 1:
                            last.then_inc(down_done, 1)

            pe.wait_ge(rows_in, 16 * 8)
            pe.wait_ge(consts, 2)
            nc.tensor.transpose(up_ps[0][:, 0:NROWS], rows[0:NROWS, :], ident[0:NROWS, 0:NROWS]).then_inc(vec_ps, 1)
            transposes(0)
            pe.wait_ge(wx0_in, 16)
            pe.wait_ge(xT_ready, 1)
            for m in range(HALVES):
                for gate in range(GATES):
                    for k in range(HALVES):
                        last = x_products(wx[0], xT[:, 0], m, gate, k)
                last.then_inc(xz_ps, 1)
            pe.wait_ge(wh_split, 1)

            def body_a(i, first):
                for s in range(PASS):
                    slot, parity = s % BLOCK, s // BLOCK
                    if lstm_on(i):
                        if slot == 0:
                            pe.wait_ge(xz_ready, 2 * (2 * i + parity) + 2)
                        lstm_step(PASS * i + s, 1, s % 2, xz[:, parity, slot], first and s == 0)
                    r = rnn_at(i, s)
                    if r is not None:
                        if first and r[2] == 0:
                            pe.wait_ge(w1_in, 32)
                        rnn_step(*r)
                    if lstm_on(i):
                        n = 2 * i + parity + 1
                        if slot == 3:
                            transposes(n)
                        if slot == 5:
                            pe.wait_ge(xT_ready, n + 1)
                        if 5 <= slot < 13:
                            m, gate = (slot - 5) // GATES, (slot - 5) % GATES
                            for k in range(HALVES):
                                last = x_products(wx[0], xT[:, 1 - parity], m, gate, k)
                            if gate == GATES - 1:
                                last.then_inc(xz_ps, 1)
                    moe = moe_at(i, s)
                    if moe is not None:
                        moe_products(*moe)

            passes(pe, body_a, lambda: pe.wait_ge(moe_in, 16 * 2 * NE))

            pe.wait_ge(gate_in_sem, 64)
            pe.wait_ge(xz_ready, 2 * (BLOCKS + 1))
            pe.wait_ge(g_dve, 1)
            for n in range(3 * HALVES):
                mm(bulk[0][0:B, 0:E], gate_in[:, n // HALVES, n % HALVES, :], gate_w_sb[:, n, :], n == 0, False)
            mm(bulk[0][0:B, 0:E], ones[0:1, 0:B], gate_b_sb[0:1, :], False, True)
            for n in range(HALVES):
                mm(bulk[1][0:B, 0:2 * E], silu[:, n * B:(n + 1) * B], time_w_sb[:, n, :], n == 0, False)
            mm(bulk[1][0:B, 0:2 * E], ones[0:1, 0:B], time_b_sb[0:1, :], False, True).then_inc(g_pe, 1)
            pe.wait_ge(g_dve, 2)
            mm(bulk[0][:, 0:E * B], ones[0:B, :], spread[:].rearrange("p e b -> p (e b)"), True, True).then_inc(g_pe, 1)

            XZ0 = 2 * (BLOCKS + 1)
            pe.wait_ge(wx3_in, 16)
            pe.wait_ge(wb_ready, 1)
            pe.wait_ge(x2_ready, 1)
            for m in range(HALVES):
                for gate in range(GATES):
                    for k in range(HALVES):
                        last = x_products(wx[3], x2[:, 0], m, gate, k)
                last.then_inc(xz_ps, 1)
            pe.wait_ge(wh_split, 2)

            def out_transposes(n):
                pe.wait_ge(x3_ready, n + 1)
                if not (isinstance(n, int) and n == 0):
                    pe.wait_ge(out_ready, n)
                for k in range(HALVES):
                    last = nc.tensor.transpose(down_ps[:, k * P:(k + 1) * P], x3[:, k].rearrange("p b t -> p (b t)"),
                                               ident[:])
                last.then_inc(out_ps, 1)

            def body_b(i, last_pass):
                for s in range(PASS):
                    slot, parity = s % BLOCK, s // BLOCK
                    n = 2 * i + parity + 1
                    if slot == 0:
                        pe.wait_ge(xz_ready, XZ0 + 2 * n)
                    lstm_step(T + PASS * i + s, 2, s % 2, xz[:, parity, slot], False)
                    if slot == 1 and not (isinstance(i, int) and i == 0 and s < BLOCK):
                        out_transposes(n - 2)
                    if not (last_pass and parity == 1):
                        if slot == 4:
                            pe.wait_ge(x2_ready, n + 1)
                        if 4 <= slot < 12:
                            m, gate = (slot - 4) // GATES, (slot - 4) % GATES
                            for k in range(HALVES):
                                last = x_products(wx[3], x2[:, 1 - parity], m, gate, k)
                            if gate == GATES - 1:
                                last.then_inc(xz_ps, 1)

            body_b(0, False)
            with pe.Fori(1, PASSES - 1) as i:
                body_b(i, False)
            body_b(PASSES - 1, True)
            out_transposes(BLOCKS - 1)

        @block.scalar
        def _(act):
            def lstm_gates(step, m):
                act.wait_ge(z_ready[m], step + 1)
                nc.scalar.activation(gc[:, m, 0:B], z[m][:, 0:B], ACT.Tanh).then_inc(gates_ready[m], 1)
                nc.scalar.activation(sig[:, m], z[m][:, B:GATES * B], ACT.Sigmoid).then_inc(gates_ready[m], 1)

            def lstm_cell(step, m):
                act.wait_ge(cell_ready[m], step + 1)
                nc.scalar.activation(tanh_c[:, m], gc[:, m, B:2 * B], ACT.Tanh).then_inc(cell_tanh[m], 1)

            def lstm_step(step):
                lstm_gates(step, 0)
                lstm_cell(step, 0)
                lstm_gates(step, 1)
                lstm_cell(step, 1)

            def body_a(i, first):
                for s in range(PASS):
                    if lstm_on(i):
                        lstm_step(PASS * i + s)
                    r = rnn_at(i, s)
                    if r is not None:
                        slot, parity, done, c = r
                        act.wait_ge(rnn_z, done + 1)
                        if slot == 0 and not (isinstance(c, int) and c < 2):
                            act.wait_ge(x1_ready, c - 1)
                        nc.scalar.activation(rnn_h[:, parity, slot].rearrange("p h b -> p (h b)"), z1[:, 0:COLS],
                                             ACT.Tanh).then_inc(rnn_h_ready, 1)
                    moe = moe_at(i, s)
                    if moe is not None:
                        w, c, parity = moe
                        for q in range(GROUPS):
                            if w == last_step[("up", q)] + 1:
                                act.wait_ge(poly_done, GROUPS * c + q + 1)
                                nc.scalar.activation(inner[:, q % 2], inner[:, q % 2], ACT.Tanh,
                                                     scale=TANH_SCALE).then_inc(th_done, 1)
                        for e in range(NE):
                            q = GPE * (e + 1) - 1
                            if w == last_step[("down", q)]:
                                act.wait_ge(down_done, NE * c + e + 1)
                                if not (isinstance(c, int) and c == 0):
                                    act.wait_ge(y_stored[e], 16 * c)
                                for m in range(HALVES):
                                    bias = column("eb2", HALVES * e + m) if e < E else column("sb2", m)
                                    nc.scalar.activation(y[:, e, :, m, :],
                                                         down_ps[:, m * TOK:(m + 1) * TOK].rearrange(
                                                             "p (t b) -> p t b", b=B),
                                                         ACT.Identity, bias=bias, scale=0.5).then_inc(y_evac, 1)
                        for q in range(GROUPS):
                            if w == last_step[("up", q)]:
                                act.wait_ge(u_ready, GROUPS * c + q + 1)
                                if q >= 1:
                                    act.wait_ge(hid_ready, GROUPS * c + q - 1)
                                nc.scalar.activation(inner[:, q % 2], u[:, q % 4], ACT.Square,
                                                     scale=CUBIC ** 0.5).then_inc(sq_ready, 1)

            act.wait_ge(vec_ready, 1)
            nc.scalar.activation(silu[:], columns("cond", COLS), ACT.Sigmoid).then_inc(g_act, 1)
            passes(act, body_a)

            act.wait_ge(g_shifted, 1)
            nc.scalar.activation(gs[:, 12:16], gs[:, 8:12], ACT.Exp).then_inc(g_act, 1)

            def body_b(i):
                for s in range(PASS):
                    lstm_step(T + PASS * i + s)

            with act.Fori(0, PASSES) as i:
                body_b(i)

        @block.vector
        def _(dve):
            def split_weights(n):
                nc.vector.tensor_copy(wh_hi[:], wh[:]).then_inc(wh_step, 1)
                dve.wait_ge(wh_step, n)
                nc.vector.tensor_tensor(wh_lo[:], wh[:], wh_hi[:].bitcast(F32), ALU.subtract).then_inc(wh_split, 1)

            def start_lstm(step):
                for m in range(HALVES):
                    src = columns("cond", COLS).rearrange("p (b h) -> p h b", h=HALVES)[:, m]
                    nc.vector.memset(gc[:, m, B:2 * B], 0.0).then_inc(full_ready[m], 1)
                    nc.vector.tensor_copy(h_hi[:, 1, m], src).then_inc(hi_ready[m], 1)
                    dve.wait_ge(hi_ready[m], step + 1)
                    dve.wait_ge(full_ready[m], step + 1)
                    nc.vector.tensor_tensor(h_lo[:, 1, m], src, h_hi[:, 1, m].bitcast(F32),
                                            ALU.subtract).then_inc(lo_ready[m], 1)

            def lstm_half(step, starts, slot, slot_parity, m):
                dve.wait_ge(gates_ready[m], 2 * (step + 1))
                nc.vector.tensor_tensor(prod[:, m], sig[:, m, 0:2 * B], gc[:, m], ALU.mult).then_inc(prod_ready[m], 1)
                dve.wait_ge(prod_ready[m], step + 1)
                nc.vector.tensor_tensor(gc[:, m, B:2 * B], prod[:, m, 0:B], prod[:, m, B:2 * B],
                                        ALU.add).then_inc(cell_ready[m], 1)
                dve.wait_ge(cell_tanh[m], step + 1)
                o = sig[:, m, 2 * B:3 * B]
                nc.vector.tensor_tensor(h_hi[:, slot_parity, m], o, tanh_c[:, m], ALU.mult).then_inc(hi_ready[m], 1)
                nc.vector.tensor_tensor(h_seq[:, slot, m], o, tanh_c[:, m], ALU.mult).then_inc(full_ready[m], 1)
                dve.wait_ge(hi_ready[m], step + 1 + starts)
                dve.wait_ge(full_ready[m], step + 1 + starts)
                nc.vector.tensor_tensor(h_lo[:, slot_parity, m], h_seq[:, slot, m],
                                        h_hi[:, slot_parity, m].bitcast(F32), ALU.subtract).then_inc(lo_ready[m], 1)

            def take_xT(n, parity):
                dve.wait_ge(xT_ps, n + 1)
                for k in range(HALVES):
                    last = nc.vector.tensor_copy(
                        xT[:, parity, :, k, :],
                        bulk[0][:, k * TOK:(k + 1) * TOK].rearrange("p (b t) -> p t b", t=BLOCK))
                last.then_inc(xT_ready, 1)

            def take_xz(count, parity, m, bias):
                dve.wait_ge(xz_ps, count)
                for gate in range(GATES):
                    last = nc.vector.tensor_scalar(
                        xz[:, parity, :, m, gate, :],
                        bulk[m][:, gate * TOK:(gate + 1) * TOK].rearrange("p (t b) -> p t b", b=B),
                        column(bias, HALVES * GATE_COLUMN[gate] + m), None, ALU.add)
                last.then_inc(xz_ready, 1)

            dve.wait_ge(vec_ps, 1)
            nc.vector.tensor_copy(vec[:, 0:NROWS], up_ps[0][:, 0:NROWS]).then_inc(vec_ready, 1)
            take_xT(0, 0)
            dve.wait_ge(wh0_in, 16)
            split_weights(1)
            dve.wait_ge(vec_ready, 1)
            start_lstm(0)
            nc.vector.tensor_copy(rnn_h[:, 1, BLOCK - 1],
                                  columns("cond", COLS).rearrange("p (b h) -> p h b", h=HALVES)).then_inc(rnn_h_ready, 1)
            take_xz(1, 0, 0, "L0_b")
            take_xz(2, 0, 1, "L0_b")

            def body_a(i, first):
                for s in range(PASS):
                    slot, parity = s % BLOCK, s // BLOCK
                    if lstm_on(i):
                        n = 2 * i + parity + 1
                        for m in range(HALVES):
                            lstm_half(PASS * i + s, 1, slot, s % 2, m)
                        if slot == 4:
                            take_xT(n, 1 - parity)
                        if slot == 9:
                            take_xz(2 * n + 1, 1 - parity, 0, "L0_b")
                        if slot == 13:
                            take_xz(2 * n + 2, 1 - parity, 1, "L0_b")
                        if slot == BLOCK - 1:
                            for m in range(HALVES):
                                dve.wait_ge(full_ready[m], PASS * i + s + 2)
                            nc.vector.tensor_tensor(rnn_x[:, parity], xT[:, parity], h_seq[:],
                                                    ALU.add).then_inc(rnn_x_ready, 1)
                    r = rnn_at(i, s)
                    if r is not None:
                        rslot, rparity, done, c = r
                        if rslot == 0:
                            dve.wait_ge(rnn_xz_ps, c + 1)
                            for m in range(HALVES):
                                last = nc.vector.tensor_scalar(
                                    rnn_xz[:, rparity, :, m, :],
                                    z1[:, COLS + m * TOK:COLS + (m + 1) * TOK].rearrange("p (t b) -> p t b", b=B),
                                    column("L1_b", m), None, ALU.add)
                            last.then_inc(rnn_xz_ready, 1)
                    r = rnn_at(i, s - 1) if passed(i, s, RNN_LAG + 1) else None
                    if r is not None and r[0] == BLOCK - 1:
                        _, rparity, done, c = r
                        dve.wait_ge(rnn_h_ready, done + 2)
                        dve.wait_ge(y_shared, c)
                        nc.vector.tensor_tensor(x1[:, rparity], rnn_x[:, rparity], rnn_h[:, rparity],
                                                ALU.add).then_inc(x1_ready, 1)
                    moe = moe_at(i, s)
                    if moe is not None:
                        w, c, _ = moe
                        for q in range(GROUPS):
                            if w == last_step[("up", q)] + 1:
                                dve.wait_ge(th_done, GROUPS * c + q + 1)
                                nc.vector.scalar_tensor_tensor(hid[:, q % 4], inner[:, q % 2], 1.0, u[:, q % 4],
                                                               ALU.add, ALU.mult).then_inc(hid_ready, 1)
                        for q in range(GROUPS):
                            if w == last_step[("up", q)]:
                                dve.wait_ge(up_done, GROUPS * c + q + 1)
                                e, g = q // GPE, q % GPE
                                bias = bias_over("eb1", GROUP, e * TILES + g * GROUP) if e < E else \
                                    bias_over("sb1", GROUP, g * GROUP)
                                nc.vector.tensor_tensor(u[:, q % 4].rearrange("p (j n) -> p j n", j=GROUP),
                                                        up_ps[q % 2][:].rearrange("p (j n) -> p j n", j=GROUP),
                                                        bias, ALU.add).then_inc(u_ready, 1)

            passes(dve, body_a)

            gate_steps = [0]

            def then(ins):
                gate_steps[0] += 1
                ins.then_inc(g_chain, 1)
                dve.wait_ge(g_chain, gate_steps[0])

            dve.wait_ge(x1_kept, BLOCKS)
            for n, (a, b_) in enumerate(SPANS):
                last = nc.vector.reduce_sum(sums[:, n].rearrange("p h b -> p (h b)"),
                                            x1_all[:, a:b_].rearrange("p t h b -> p (h b) t"), AX_X)
            then(last)
            head, wrist, proprio = (sums[:, n] for n in range(3))
            lengths = [b_ - a for a, b_ in SPANS]
            then(nc.vector.tensor_tensor(gate_in[:, 1], head, proprio, ALU.add))
            then(nc.vector.tensor_tensor(gate_in[:, 2], wrist, proprio, ALU.add))
            then(nc.vector.tensor_tensor(gate_in[:, 0], gate_in[:, 1], wrist, ALU.add))
            then(nc.vector.tensor_scalar(gate_in[:, 0], gate_in[:, 0], 1.0 / T, None, ALU.mult))
            then(nc.vector.tensor_scalar(gate_in[:, 1], gate_in[:, 1], 1.0 / (lengths[0] + lengths[2]), None, ALU.mult))
            then(nc.vector.tensor_scalar(gate_in[:, 2], gate_in[:, 2], 1.0 / (lengths[1] + lengths[2]), None, ALU.mult))
            dve.wait_ge(g_act, 1)
            then(nc.vector.tensor_tensor(gtmp[:], silu[:], columns("cond", COLS), ALU.mult))
            nc.vector.tensor_copy(silu[:].rearrange("p (h b) -> p h b", h=HALVES),
                                  gtmp[:].rearrange("p (b h) -> p h b", h=HALVES)).then_inc(g_dve, 1)
            dve.wait_ge(g_pe, 1)
            mod, logits, shifted, expd = gs[:, 0:8], gs[:, 16:20], gs[:, 8:12], gs[:, 12:16]
            score, rank, top, wgt = gs[:, 20:24], gs[:, 24:28], gs[:, 28:32], gs[:, 32:36]
            one = gs[:, 40:41]
            then(nc.vector.tensor_copy(mod, bulk[1][0:B, 0:2 * E]))
            then(nc.vector.tensor_scalar(mod[:, 0:E], mod[:, 0:E], 1.0, None, ALU.add))
            then(nc.vector.tensor_tensor(logits, bulk[0][0:B, 0:E], mod[:, 0:E], ALU.mult))
            then(nc.vector.tensor_tensor(logits, logits, mod[:, E:2 * E], ALU.add))
            then(nc.vector.reduce_max(one, logits, AX_X))
            nc.vector.tensor_scalar(shifted, logits, one, None, ALU.subtract).then_inc(g_shifted, 1)
            dve.wait_ge(g_act, 2)
            then(nc.vector.reduce_sum(gs[:, 41:42], expd, AX_X))
            then(nc.vector.reciprocal(gs[:, 42:43], gs[:, 41:42]))
            then(nc.vector.tensor_scalar(score, expd, gs[:, 42:43], None, ALU.mult))
            then(nc.vector.memset(rank, 0.0))
            for j in range(E):
                s_j = score[:, j:j + 1]
                if j > 0:
                    then(nc.vector.scalar_tensor_tensor(rank[:, 0:j], score[:, 0:j], s_j, rank[:, 0:j],
                                                        ALU.is_lt, ALU.add))
                if j < E - 1:
                    then(nc.vector.scalar_tensor_tensor(rank[:, j + 1:E], score[:, j + 1:E], s_j, rank[:, j + 1:E],
                                                        ALU.is_le, ALU.add))
            then(nc.vector.scalar_tensor_tensor(top, rank, 2.0, score, ALU.is_lt, ALU.mult))
            then(nc.vector.reduce_sum(gs[:, 43:44], top, AX_X))
            then(nc.vector.tensor_scalar(gs[:, 44:45], gs[:, 43:44], 1e-8, None, ALU.add))
            then(nc.vector.reciprocal(gs[:, 45:46], gs[:, 44:45]))
            then(nc.vector.tensor_scalar(wgt, top, gs[:, 45:46], None, ALU.mult))
            nc.vector.tensor_tensor(spread[:], wgt[:, :, None].to_broadcast([B, E, B]),
                                    ident[0:B, None, 0:B].to_broadcast([B, E, B]), ALU.mult).then_inc(g_dve, 1)
            dve.wait_ge(g_pe, 2)
            nc.vector.tensor_copy(wb[:].rearrange("p e b -> p (e b)"), bulk[0][:, 0:E * B]).then_inc(wb_ready, 1)
            dve.wait_ge(wh3_in, 16)
            split_weights(2)
            start_lstm(T + 1)

            XZ0 = 2 * (BLOCKS + 1)
            take_xz(XZ0 + 1, 0, 0, "L3_b")
            take_xz(XZ0 + 2, 0, 1, "L3_b")

            def body_b(i, last_pass):
                for s in range(PASS):
                    slot, parity = s % BLOCK, s // BLOCK
                    n = 2 * i + parity + 1
                    for m in range(HALVES):
                        lstm_half(T + PASS * i + s, 2, slot, s % 2, m)
                    if slot == BLOCK - 1:
                        for m in range(HALVES):
                            dve.wait_ge(full_ready[m], T + PASS * i + s + 3)
                        if not (isinstance(i, int) and i == 0 and parity == 0):
                            dve.wait_ge(out_ps, n - 1)
                        for m in range(HALVES):
                            last = nc.vector.tensor_tensor(x3[:, m], x2[:, parity, :, m, :].rearrange("p t b -> p b t"),
                                                           h_seq[:, :, m, :].rearrange("p t b -> p b t"), ALU.add)
                        last.then_inc(x3_ready, 1)
                    if slot == 2 and not (isinstance(i, int) and i == 0 and parity == 0):
                        take_out(n - 2)
                    if not (last_pass and parity == 1):
                        if slot == 8:
                            take_xz(XZ0 + 2 * n + 1, 1 - parity, 0, "L3_b")
                        if slot == 12:
                            take_xz(XZ0 + 2 * n + 2, 1 - parity, 1, "L3_b")

            def take_out(n):
                dve.wait_ge(out_ps, n + 1)
                if not (isinstance(n, int) and n == 0):
                    dve.wait_ge(stored, 16 * n)
                nc.vector.tensor_copy(out_rows[:], down_ps[:, 0:D]).then_inc(out_ready, 1)

            body_b(0, False)
            with dve.Fori(1, PASSES - 1) as i:
                body_b(i, False)
            body_b(PASSES - 1, True)
            take_out(BLOCKS - 1)

        @block.gpsimd
        def _(pool):
            nc.gpsimd.memset(ident[:], 0.0).then_inc(pool_c, 1)
            nc.gpsimd.memset(ones[:], 1.0).then_inc(consts, 1)
            pool.wait_ge(pool_c, 1)
            nc.gpsimd.affine_select(out=ident[:], in_=ident[:], compare_op=ALU.not_equal, fill=1.0, base=0,
                                    pattern=[[-1, P]], channel_multiplier=1).then_inc(consts, 1)
            nc.gpsimd.memset(keep[:], 1.0).then_inc(pool_c, 1)
            pool.wait_ge(pool_c, 2)
            nc.gpsimd.memset(keep[:, 0, THIRD:2 * THIRD], 0.0).then_inc(pool_c, 1)
            nc.gpsimd.memset(keep[:, 1, 0:THIRD], 0.0).then_inc(y_shared, 1)
            pool.wait_ge(pool_c, 3)
            pool.wait_ge(y_shared, 1)

            def body_a(i, first):
                for s in range(PASS):
                    moe = moe_at(i, s)
                    if moe is not None:
                        w, c, parity = moe
                        if w == 0:
                            pool.wait_ge(x1_ready, c + 1)
                            nc.gpsimd.tensor_copy(x1_all[:, bass.ds(c * BLOCK, BLOCK)].rearrange("p t h b -> p (t h b)"),
                                                  x1[:, parity].rearrange("p t h b -> p (t h b)")).then_inc(x1_kept, 1)
                        for e in (1, 2, E):
                            if w == last_step[("down", GPE * (e + 1) - 1)]:
                                pool.wait_ge(y_evac, 2 * (NE * c + e + 1))
                                if e < E:
                                    mask = keep[:, e - 1, bass.ds(c * BLOCK, BLOCK)]
                                    nc.gpsimd.tensor_tensor(
                                        y[:, e].rearrange("p t h b -> p t (h b)"),
                                        y[:, e].rearrange("p t h b -> p t (h b)"),
                                        mask[:, :, None].to_broadcast([P, BLOCK, COLS]), ALU.mult).then_inc(y_masked, 1)
                                else:
                                    pool.wait_ge(x1_kept, c + 1)
                                    nc.gpsimd.tensor_tensor(y[:, e], y[:, e], x1[:, parity],
                                                            ALU.add).then_inc(y_shared, 1)
                        for q in range(GROUPS):
                            if w == last_step[("up", q)]:
                                n = GROUPS * c + q
                                pool.wait_ge(sq_ready, n + 1)
                                v = inner[:, q % 2]
                                nc.gpsimd.tensor_tensor(v, v, u[:, q % 4], ALU.mult).then_inc(pool_chain, 1)
                                pool.wait_ge(pool_chain, n + 1)
                                nc.gpsimd.tensor_tensor(v, v, u[:, q % 4], ALU.add).then_inc(poly_done, 1)

            passes(pool, body_a)

            def combine(n, parity):
                pool.wait_ge(y_loaded, 16 * NE * (n + 1))
                acc = x2[:, parity].rearrange("p t h b -> p (t h) b")
                for e in range(E):
                    if e:
                        pool.wait_ge(x2_chain, 7 * n + 2 * e)
                    else:
                        pool.wait_ge(x2_ready, n)
                    nc.gpsimd.tensor_tensor(part[:].rearrange("p t h b -> p (t h) b"),
                                            y_back[:, e].rearrange("p t h b -> p (t h) b"),
                                            wb[:, e, None, :].to_broadcast([P, 2 * BLOCK, B]),
                                            ALU.mult).then_inc(x2_chain, 1)
                    pool.wait_ge(x2_chain, 7 * n + 2 * e + 1)
                    base = y_back[:, E].rearrange("p t h b -> p (t h) b") if e == 0 else acc
                    last = nc.gpsimd.tensor_tensor(acc, base, part[:].rearrange("p t h b -> p (t h) b"), ALU.add)
                    last.then_inc(x2_chain if e < E - 1 else x2_ready, 1)

            pool.wait_ge(wb_ready, 1)
            combine(0, 0)

            def body_b(i, last_pass):
                for parity in range(2):
                    if not (last_pass and parity == 1):
                        n = 2 * i + parity + 1
                        if not (isinstance(n, int) and n < 2):
                            pool.wait_ge(x3_ready, n - 1)
                        combine(n, 1 - parity)

            body_b(0, False)
            with pool.Fori(1, PASSES - 1) as i:
                body_b(i, False)
            body_b(PASSES - 1, True)


_INS = ["x", "cond_1024", "L0_cond_Wx", "L0_cond_Wh", "L0_cond_b", "L1_cond_Wx", "L1_cond_Wh", "L1_cond_b",
        "L2_cond_gate_w", "L2_cond_gate_b", "L2_cond_time_w", "L2_cond_time_b", "L2_cond_ew1", "L2_cond_eb1",
        "L2_cond_ew2", "L2_cond_eb2", "L2_cond_sw1", "L2_cond_sb1", "L2_cond_sw2", "L2_cond_sb2",
        "L3_cond_Wx", "L3_cond_Wh", "L3_cond_b"]


def kernel(**inputs):
    import numpy as _np
    import concourse.bacc as _bacc
    from concourse import mybir as _mybir
    from concourse.bass_utils import run_bass_kernel_spmd as _run

    nc = _bacc.Bacc("TRN2", target_bir_lowering=False, num_devices=1)
    arrays, args = {}, []
    for name in _INS:
        a = _np.ascontiguousarray(inputs[name])
        arrays[f"in_{name}_dram"] = a
        args.append(nc.dram_tensor(f"in_{name}_dram", a.shape, _mybir.dt.from_np(a.dtype), kind="ExternalInput").ap())
    out = nc.dram_tensor("out_dram", (8, 256, 256), _mybir.dt.float32, kind="ExternalOutput").ap()
    cond_residual_kernel(nc, *args, out)
    r = _run(nc, [arrays], core_ids=[0])
    return r.results[0]["out_dram"]
```

```python
from contextlib import ExitStack

import concourse.bass as bass
from concourse import mybir

F32 = mybir.dt.float32
F16 = mybir.dt.float16
I32 = mybir.dt.int32
ALU = mybir.AluOpType
ACT = mybir.ActivationFunctionType
AX_X = mybir.AxisListType.X

P = 128
HALVES = 2
GATES = 4
PARTS = 2
GATE_COLUMN = (3, 0, 1, 2)
BLOCK = 32
PASS = 2 * BLOCK
GROUP = 2
TANH_SCALE = 0.7978845608028654
CUBIC = 0.044715
H_SCALE = 256.0
W_TOP = 2.0 ** 14


def cond_residual_kernel(nc, x, cond_1024, L0_Wx, L0_Wh, L0_b, L1_Wx, L1_Wh, L1_b, gate_w, gate_b, time_w, time_b,
                         ew1, eb1, ew2, eb2, sw1, sb1, sw2, sb2, L3_Wx, L3_Wh, L3_b, out):
    B, T, D = x.shape
    E, _, H = ew1.shape
    assert D == HALVES * P and B == 8 and T % PASS == 0 and L0_Wh.shape == (D, GATES * D)
    PASSES = T // PASS
    BLOCKS = T // BLOCK
    TOK = BLOCK * B
    COLS = HALVES * B
    NE = E + 1
    TILES = H // P
    GPE = TILES // GROUP
    GROUPS = NE * GPE
    THIRD = T // 3
    SPANS = ((0, THIRD), (THIRD, 2 * THIRD), (2 * THIRD, T))
    FILLS = HALVES * GATES // 2
    BANK = 2 * TOK
    assert BANK == 512 and GROUP * TOK == BANK and HALVES * TOK == BANK
    XTILES = TOK // P

    items = []
    for q in range(GROUPS + 2):
        if q < GROUPS:
            items.append(("up", q))
        if q >= 2:
            items.append(("down", q - 2))
    MM_PER_ITEM = GROUP * HALVES
    MMS = len(items) * MM_PER_ITEM

    class Window:

        def __init__(self, width):
            self.width = width
            begin = {it: n * MM_PER_ITEM * width // MMS for n, it in enumerate(items)}
            end = {it: (((n + 1) * MM_PER_ITEM - 1) * width) // MMS for n, it in enumerate(items)}
            self.up = [end["up", q] for q in range(GROUPS)]
            self.hid = [min(self.up[q] + 4, begin["down", q]) for q in range(GROUPS)]
            self.tanh = [min(self.up[q] + 3, self.hid[q]) for q in range(GROUPS)]
            self.square = [min(self.up[q] + 1, self.tanh[q]) for q in range(GROUPS)]
            self.out = [end["down", GPE * (e + 1) - 1] for e in range(NE)]

        def matmuls(self, w):
            return [n for n in range(MMS) if n * self.width // MMS == w]

    SLOW, FAST = Window(PASS), Window(BLOCK)

    ROWS = {}
    at = 0
    for name, rows_ in (("eb1", E * TILES), ("sb1", TILES), ("eb2", E * HALVES), ("sb2", HALVES),
                        ("L0_b", GATES * HALVES), ("L1_b", HALVES), ("L3_b", GATES * HALVES), ("cond", B * HALVES)):
        ROWS[name] = at
        at += rows_
    NROWS = at

    with ExitStack() as ctx:
        def sb(name, shape, dt=F32):
            return ctx.enter_context(nc.sbuf_tensor(name, shape, dt))

        def psum(name):
            return ctx.enter_context(nc.psum_tensor(name, [P, 512], F32))

        def sem(name):
            return ctx.enter_context(nc.semaphore(name))

        wx = sb("wx", [P, HALVES, GATES * D])
        wh = sb("wh", [P, HALVES, GATES * D])
        wh16 = sb("wh16", [P, PARTS, HALVES, GATES * D], F16)
        wx1 = sb("wx1", [P, HALVES, D])
        wh1 = sb("wh1", [P, HALVES, D])
        wh1_16 = sb("wh1_16", [P, PARTS, HALVES, D], F16)
        up_w = sb("up_w", [P, NE, HALVES, H])
        down_w = sb("down_w", [P, NE, TILES, D])
        rows = sb("rows", [P, P])
        vec = sb("vec", [P, P])
        gate_w_sb = sb("gate_w_sb", [P, 3 * HALVES, E])
        time_w_sb = sb("time_w_sb", [P, HALVES, 2 * E])
        gate_b_sb = sb("gate_b_sb", [1, E])
        time_b_sb = sb("time_b_sb", [1, 2 * E])
        ident = sb("ident", [P, P])
        ones = sb("ones", [P, P])
        keep = sb("keep", [P, 2, T])
        w_max = sb("w_max", [P, 3])
        w_top = sb("w_top", [P, 3])
        w_pow = sb("w_pow", [P, 3])
        w_inv = sb("w_inv", [P, 3])
        up_scale = sb("up_scale", [P, 3])
        unscale = sb("unscale", [P, 3])
        x_rows = sb("x_rows", [P, XTILES, D])
        xT = sb("xT", [P, 2, BLOCK, HALVES, B])
        xz = sb("xz", [P, 2, BLOCK, HALVES, GATES, B])
        h_seq = sb("h_seq", [P, BLOCK, HALVES, B])
        h16 = sb("h16", [P, HALVES, PARTS, B], F16)
        zt = sb("zt", [P, HALVES, GATES, B])
        zs = sb("zs", [P, HALVES, GATES, B])
        sig = sb("sig", [P, HALVES, 3, B])
        gc = sb("gc", [P, HALVES, 2, B])
        prod = sb("prod", [P, HALVES, 2, B])
        tanh_c = sb("tanh_c", [P, HALVES, B])
        rnn_x = sb("rnn_x", [P, 2, BLOCK, HALVES, B])
        rnn_xz = sb("rnn_xz", [P, BLOCK, HALVES, B])
        rnn_h = sb("rnn_h", [P, 2, BLOCK, HALVES, B])
        rnn_h16 = sb("rnn_h16", [P, HALVES, PARTS, B], F16)
        first_rnn = sb("first_rnn", [P, COLS])
        first_h3 = sb("first_h3", [P, GATES * COLS])
        rnn_zt = sb("rnn_zt", [P, HALVES, B])
        rnn_zs = sb("rnn_zs", [P, HALVES, B])
        x1 = sb("x1", [P, T, HALVES, B])
        u = sb("u", [P, 4, BANK])
        inner = sb("inner", [P, 2, BANK])
        hid = sb("hid", [P, 4, BANK])
        y = sb("y", [P, NE, BLOCK, HALVES, B])
        sums = sb("sums", [P, 3, HALVES, B])
        gate_in = sb("gate_in", [P, 3, HALVES, B])
        gtmp = sb("gtmp", [P, COLS])
        silu = sb("silu", [P, COLS])
        gs = sb("gs", [B, 64])
        spread = sb("spread", [B, E, B])
        wb = sb("wb", [P, E, B])
        whf = wh[:].rearrange("p k n -> p (k n)")
        y_back = whf[:, 0:2 * BANK].rearrange("p (a t h b) -> p a t h b", a=2, h=HALVES, b=B)
        x2 = whf[:, 2 * BANK:4 * BANK].rearrange("p (a t h b) -> p a t h b", a=2, h=HALVES, b=B)
        part = sb("part", [P, BLOCK, HALVES, B])
        x3 = sb("x3", [P, HALVES, B, BLOCK])
        out_rows = sb("out_rows", [P, XTILES, D])

        z = psum("z")
        z1 = psum("z_rnn")
        up_ps = [psum("up0"), psum("up1")]
        down_ps = psum("down")
        bulk = [psum("bulk0"), psum("bulk1")]
        spare = psum("spare")

        y_dram = nc.dram_tensor("expert_out", [BLOCKS, 1 + NE, P, BANK], F32, kind="Internal").ap()

        rows_in, x_in, wx_in, wh_in, w1_in, gate_params_in = (
            sem(n) for n in ("rows_in", "x_in", "wx_in", "wh_in", "w1_in", "gate_params_in"))
        expert_dma = [sem(f"expert_dma{e}") for e in range(NE)]
        consts, pool_c = sem("consts"), sem("pool_consts")
        vec_ps, vec_ready = sem("vec_ps"), sem("vec_ready")
        w_max_ready, w_top_ready, w_chain, wh_split, wh1_split = (
            sem(n) for n in ("w_max_ready", "w_top_ready", "w_chain", "wh_split", "wh1_split"))
        h0_z, h0_added, first_rnn_ready = sem("h0_z"), sem("h0_added"), sem("first_rnn_ready")
        xT_ps, xT_ready, xz_ps, xz_ready = sem("xT_ps"), sem("xT_ready"), sem("xz_ps"), sem("xz_ready")
        z_ready, zt_ready, zs_ready, gates_ready, prod_ready, cell_ready, cell_tanh, h1_ready, full_ready, h_ready = (
            sem(n) for n in ("z_ready", "zt_ready", "zs_ready", "gates_ready", "prod_ready", "cell_ready",
                             "cell_tanh", "h1_ready", "full_ready", "h_ready"))
        rnn_x_ready, rnn_xz_ps, rnn_xz_ready = sem("rnn_x_ready"), sem("rnn_xz_ps"), sem("rnn_xz_ready")
        rnn_z_ready, rnn_zt_ready, rnn_zs_ready, rnn_tanh, rnn_h1_ready, rnn_h_ready = (
            sem(n) for n in ("rnn_z_ready", "rnn_zt_ready", "rnn_zs_ready", "rnn_tanh", "rnn_h1_ready", "rnn_h_ready"))
        x1_ready, up_done, u_ready, sq_ready, pool_chain, poly_done, th_done, hid_ready = (
            sem(n) for n in ("x1_ready", "up_done", "u_ready", "sq_ready", "pool_chain", "poly_done", "th_done",
                             "hid_ready"))
        down_done, y_evac, y_masked, y_shared = sem("down_done"), sem("y_evac"), sem("y_masked"), sem("y_shared")
        g_dve, g_act, g_pe, g_chain, g_shifted = (
            sem(n) for n in ("gate_dve", "gate_act", "gate_pe", "gate_chain", "gate_shifted"))
        wb_ready = sem("wb_ready")
        y_loaded = [sem("y_loaded0"), sem("y_loaded1")]
        x2_part, x2_sum = sem("x2_part"), sem("x2_sum")
        x3_ready, out_ps, out_ready, stored = sem("x3_ready"), sem("out_ps"), sem("out_ready"), sem("stored")

        block = ctx.enter_context(nc.Block())

        def column(name, n=0):
            return vec[:, ROWS[name] + n:ROWS[name] + n + 1]

        def columns(name, n, start=0):
            return vec[:, ROWS[name] + start:ROWS[name] + start + n]

        def bias_over(name, n, start):
            return columns(name, n, start)[:, :, None].to_broadcast([P, n, TOK])

        def cond_T():
            return columns("cond", COLS).rearrange("p (b h) -> p h b", h=HALVES)

        def lstm_at(i):
            return not (isinstance(i, int) and i == PASSES)

        def rnn_at(i, s):
            if isinstance(i, int) and not 0 <= PASS * i + s - BLOCK < T:
                return None
            t = s - BLOCK
            return t % BLOCK, (t // BLOCK) % 2, i * PASS + t, 2 * i + t // BLOCK

        def experts_a(i, s):
            if isinstance(i, int) and i == 0:
                return None
            if isinstance(i, int) and i == PASSES:
                return FAST, s, PASSES - 1
            return SLOW, s, i - 1

        def experts_b(i, s):
            if isinstance(i, int) and i == 0:
                return FAST, s % BLOCK, PASSES + s // BLOCK
            if isinstance(i, int) and i == PASSES - 1:
                return None
            return SLOW, s, i + PASSES + 1

        assert PASSES + 1 + PASSES - 1 == BLOCKS

        @block.sync
        def _(sp):
            def at(v):
                return v if isinstance(v, int) else sp.snap(v)

            def load_x(n):
                t, taken = at(n % BLOCKS * BLOCK), at(n)
                if not isinstance(n, int) or n > 0:
                    sp.wait_ge(xT_ps, taken)
                for j in range(XTILES):
                    half = B // XTILES
                    sp.dma_start(x_rows[:, j, :], x[half * j:half * (j + 1), bass.ds(t, BLOCK), :]
                                 ).then_inc(x_in, 16)

            load_x(0)
            for name, src in (("eb1", eb1.rearrange("e (j p) -> (e j) p", p=P)),
                              ("sb1", sb1.rearrange("(j p) -> j p", p=P)),
                              ("eb2", eb2.rearrange("e (j p) -> (e j) p", p=P)),
                              ("sb2", sb2.rearrange("(j p) -> j p", p=P)),
                              ("L1_b", L1_b.rearrange("(j p) -> j p", p=P)),
                              ("cond", cond_1024.rearrange("b (j p) -> (b j) p", p=P))):
                sp.dma_start(rows[ROWS[name]:ROWS[name] + src.shape[0], :], src).then_inc(rows_in, 16)
            for name, b_dram in (("L0_b", L0_b), ("L3_b", L3_b)):
                for gate in range(GATES):
                    c = GATE_COLUMN[gate] * D
                    for m in range(HALVES):
                        r = ROWS[name] + GATES * m + gate
                        sp.dma_start(rows[r:r + 1, :], b_dram[c + m * P:c + (m + 1) * P].rearrange("(a p) -> a p", a=1)
                                     ).then_inc(rows_in, 16)
            sp.dma_start(wh[:], L0_Wh.rearrange("(k p) n -> p k n", p=P)).then_inc(wh_in, 16)
            sp.dma_start(wx[:], L0_Wx.rearrange("(k p) n -> p k n", p=P)).then_inc(wx_in, 16)
            sp.dma_start(wh1[:], L1_Wh.rearrange("(k p) n -> p k n", p=P)).then_inc(w1_in, 16)
            sp.dma_start(wx1[:], L1_Wx.rearrange("(k p) n -> p k n", p=P)).then_inc(w1_in, 16)
            for e in range(NE):
                w1 = ew1[e] if e < E else sw1
                w2 = ew2[e] if e < E else sw2
                sp.dma_start(up_w[:, e], w1.rearrange("(k p) n -> p k n", p=P)).then_inc(expert_dma[e], 16)
                sp.dma_start(down_w[:, e], w2.rearrange("(j p) n -> p j n", p=P)).then_inc(expert_dma[e], 16)
            sp.dma_start(gate_w_sb[:], gate_w.rearrange("(k p) n -> p k n", p=P)).then_inc(gate_params_in, 16)
            sp.dma_start(time_w_sb[:], time_w.rearrange("(k p) n -> p k n", p=P)).then_inc(gate_params_in, 16)
            sp.dma_start(gate_b_sb[:], gate_b.rearrange("(a n) -> a n", a=1)).then_inc(gate_params_in, 16)
            sp.dma_start(time_b_sb[:], time_b.rearrange("(a n) -> a n", a=1)).then_inc(gate_params_in, 16)

            def store_experts(win, w, c):
                for e in range(NE):
                    if w == win.out[e]:
                        c_at = at(c)
                        if e == E:
                            written, count = y_shared, at(c + 1)
                        elif e in (1, 2):
                            written, count = y_masked, at(2 * c + e)
                        else:
                            written, count = y_evac, at(2 * (NE * c + e + 1))
                        sp.wait_ge(written, count)
                        dst = y_dram[bass.ds(c_at, 1), 1 + e].rearrange("a p n -> (a p) n")
                        sp.dma_start(dst, y[:, e].rearrange("p t h b -> p (t h b)")).then_inc(expert_dma[e], 16)

            def body_a(i):
                for s in range(PASS if lstm_at(i) else BLOCK):
                    if lstm_at(i) and s % BLOCK == 0:
                        load_x(2 * i + s // BLOCK + 1)
                    if experts_a(i, s) is not None:
                        store_experts(*experts_a(i, s))

            body_a(0)
            with sp.Fori(1, PASSES) as i:
                body_a(i)
            sp.wait_ge(xz_ps, FILLS * (BLOCKS + 1))
            sp.dma_start(wx[:], L3_Wx.rearrange("(k p) n -> p k n", p=P)).then_inc(wx_in, 16)
            sp.dma_start(wh[:], L3_Wh.rearrange("(k p) n -> p k n", p=P)).then_inc(wh_in, 16)
            body_a(PASSES)

            def load_block(n):
                n_at = at(n)
                if not (isinstance(n, int) and n == 0):
                    sp.wait_ge(x2_sum, E * n)
                stored_count = at(32 + 16 * (n + 1))
                for e in range(NE):
                    sp.wait_ge(expert_dma[e], stored_count)
                for k in range(NE):
                    if k >= 2:
                        sp.wait_ge(x2_sum, E * n + k - 1)
                    sp.dma_start(y_back[:, k % 2].rearrange("p t h b -> p (t h b)"),
                                 y_dram[bass.ds(n_at, 1), 1 + (k - 1) % NE].rearrange("a p n -> (a p) n")
                                 ).then_inc(y_loaded[k % 2], 16)

            def store(n):
                t, taken = at(n * BLOCK), at(n + 1)
                sp.wait_ge(out_ready, taken)
                half = B // XTILES
                for j in range(XTILES):
                    sp.dma_start(out[half * j:half * (j + 1), bass.ds(t, BLOCK), :],
                                 out_rows[:, j, :]).then_inc(stored, 16)

            sp.wait_ge(h0_added, 2)
            load_block(0)

            def body_b(i, first, last):
                for s in range(PASS):
                    if s % BLOCK == 0 and not (last and s == BLOCK):
                        load_block(2 * i + s // BLOCK + 1)
                    if s % BLOCK == 6 and not (first and s < BLOCK):
                        store(2 * i + s // BLOCK - 1)
                    if experts_b(i, s) is not None:
                        store_experts(*experts_b(i, s))

            body_b(0, True, False)
            with sp.Fori(1, PASSES - 1) as i:
                body_b(i, False, False)
            body_b(PASSES - 1, False, True)
            store(BLOCKS - 1)
            sp.wait_ge(stored, 16 * XTILES * BLOCKS)
            for e in range(NE):
                sp.wait_ge(expert_dma[e], 32 + 16 * BLOCKS)

        @block.tensor
        def _(pe):
            def mm(out_ap, lhsT, rhs, start, stop):
                return nc.tensor.matmul(out_ap, lhsT, rhs, start=start, stop=stop, skip_group_check=True)

            def tb(ap):
                return ap.rearrange("p (t b) -> p t b", b=B)

            def gate_column(gate, m):
                return GATE_COLUMN[gate] * D + m * P

            def transposes(n):
                pe.wait_ge(x_in, 16 * XTILES * (n + 1))
                for k in range(HALVES):
                    for j in range(XTILES):
                        last = nc.tensor.transpose(bulk[0][:, (XTILES * k + j) * P:(XTILES * k + j + 1) * P],
                                                   x_rows[:, j, k * P:(k + 1) * P], ident[:])
                last.then_inc(xT_ps, 1)

            def x_product(fill, r, rhs):
                j, k = r // HALVES, r % HALVES
                m, gate = fill // 2, 2 * (fill % 2) + j
                c = gate_column(gate, m)
                last = mm(tb(bulk[fill % 2][:, j * TOK:(j + 1) * TOK]), wx[:, k, c:c + P], rhs[:, :, k, :],
                          k == 0, k == HALVES - 1)
                if r == 2 * HALVES - 1:
                    last.then_inc(xz_ps, 1)

            def lstm_step(step, starts):
                pe.wait_ge(h_ready, step + starts)
                for k in range(HALVES):
                    for m in range(HALVES):
                        for gate in range(GATES):
                            n, c = (GATES * m + gate) * PARTS * B, gate_column(gate, m)
                            for a in range(PARTS):
                                last = mm(z[:, n:n + PARTS * B], wh16[:, a, k, c:c + P],
                                          h16[:, k].rearrange("p a b -> p (a b)"),
                                          k == m == gate == a == 0, k == a == 1)
                last.then_inc(z_ready, 1)

            def first_h(h_product):
                for m in range(HALVES):
                    for gate in range(GATES):
                        n, c = (GATES * m + gate) * B, gate_column(gate, m)
                        for k in range(HALVES):
                            last = mm(spare[:, n:n + B], wh[:, k, c:c + P], cond_T()[:, k], k == 0, k == 1)
                last.then_inc(h0_z, 1)

            def rnn_step(slot, parity, done, c):
                if slot == 0:
                    pe.wait_ge(rnn_x_ready, c + 1)
                    for m in range(HALVES):
                        for k in range(HALVES):
                            last = mm(tb(bulk[1][:, m * TOK:(m + 1) * TOK]), wx1[:, k, m * P:(m + 1) * P],
                                      rnn_x[:, parity, :, k, :], k == 0, k == 1)
                    last.then_inc(rnn_xz_ps, 1)
                pe.wait_ge(rnn_h_ready, done + 1)
                for k in range(HALVES):
                    for m in range(HALVES):
                        for a in range(PARTS):
                            last = mm(z1[:, m * PARTS * B:(m + 1) * PARTS * B], wh1_16[:, a, k, m * P:(m + 1) * P],
                                      rnn_h16[:, k].rearrange("p a b -> p (a b)"), k == m == a == 0, k == a == 1)
                last.then_inc(rnn_z_ready, 1)

            def expert_products(win, w, c):
                for n in win.matmuls(w):
                    kind, q = items[n // MM_PER_ITEM]
                    r = n % MM_PER_ITEM
                    e, g = q // GPE, q % GPE
                    if kind == "up":
                        if r == 0 and q == 0:
                            pe.wait_ge(x1_ready, c + 1)
                        if r == 0 and q >= 2:
                            pe.wait_ge(u_ready, GROUPS * c + q - 1)
                        j, k = r // HALVES, r % HALVES
                        last = mm(tb(up_ps[q % 2][:, j * TOK:(j + 1) * TOK]),
                                  up_w[:, e, k, (GROUP * g + j) * P:(GROUP * g + j + 1) * P],
                                  x1[:, bass.ds(c * BLOCK, BLOCK), k, :], k == 0, k == 1)
                        if r == MM_PER_ITEM - 1:
                            last.then_inc(up_done, 1)
                    else:
                        if r == 0:
                            pe.wait_ge(hid_ready, GROUPS * c + q + 1)
                            if g == 0 and e > 0:
                                pe.wait_ge(y_evac, 2 * (NE * c + e))
                        m, j = r // GROUP, r % GROUP
                        last = mm(down_ps[:, m * TOK:(m + 1) * TOK],
                                  down_w[:, e, GROUP * g + j, m * P:(m + 1) * P],
                                  hid[:, q % 4, j * TOK:(j + 1) * TOK], g == 0 and r == 0,
                                  g == GPE - 1 and j == GROUP - 1)
                        if r == MM_PER_ITEM - 1 and g == GPE - 1:
                            last.then_inc(down_done, 1)

            pe.wait_ge(rows_in, 16 * (6 + 2 * GATES * HALVES))
            pe.wait_ge(consts, 2)
            nc.tensor.transpose(up_ps[0][:, 0:NROWS], rows[0:NROWS, :], ident[0:NROWS, 0:NROWS]).then_inc(vec_ps, 1)
            transposes(0)
            pe.wait_ge(vec_ready, 1)
            pe.wait_ge(wh_in, 16)
            first_h(0)
            pe.wait_ge(wx_in, 16)
            pe.wait_ge(xT_ready, 1)
            for fill in range(FILLS):
                if fill >= 2:
                    pe.wait_ge(xz_ready, fill - 1)
                for r in range(2 * HALVES):
                    x_product(fill, r, xT[:, 0])
            pe.wait_ge(w1_in, 32)
            for m in range(HALVES):
                for k in range(HALVES):
                    last = mm(z1[:, m * B:(m + 1) * B], wh1[:, k, m * P:(m + 1) * P], cond_T()[:, k], k == 0, k == 1)
            last.then_inc(rnn_z_ready, 1)
            pe.wait_ge(first_rnn_ready, 1)
            pe.wait_ge(wh1_split, 1)
            pe.wait_ge(wh_split, 1)

            def next_products(n, slot, rhs, with_rnn):
                fill, r = divmod(slot - 5, 6)
                if 0 <= fill < FILLS and r < 4:
                    if r == 0:
                        if fill == 1 and with_rnn is not None:
                            pe.wait_ge(rnn_xz_ready, with_rnn + 1)
                        if fill >= 2:
                            pe.wait_ge(xz_ready, FILLS * n + fill - 1)
                    x_product(fill, r, rhs)

            def body_a(i):
                for s in range(PASS if lstm_at(i) else BLOCK):
                    slot, parity = s % BLOCK, s // BLOCK
                    if lstm_at(i):
                        lstm_step(PASS * i + s, 1)
                    if slot == 0:
                        pe.wait_ge(xz_ready, FILLS * (2 * i + parity + 1))
                    r = rnn_at(i, s)
                    if r is not None:
                        rnn_step(*r)
                    if lstm_at(i):
                        n = 2 * i + parity + 1
                        if slot == 2:
                            transposes(n)
                        if slot == 4:
                            pe.wait_ge(xT_ready, n + 1)
                        next_products(n, slot, xT[:, 1 - parity], None if r is None else r[3])
                    if experts_a(i, s) is not None:
                        expert_products(*experts_a(i, s))

            body_a(0)
            for e in range(NE):
                pe.wait_ge(expert_dma[e], 32)
            with pe.Fori(1, PASSES) as i:
                body_a(i)
            pe.wait_ge(wh_in, 32)
            first_h(1)
            body_a(PASSES)

            pe.wait_ge(gate_params_in, 64)
            pe.wait_ge(h0_added, 2)
            pe.wait_ge(rnn_xz_ready, BLOCKS)
            pe.wait_ge(g_dve, 1)
            for n in range(3 * HALVES):
                mm(spare[0:B, 0:E], gate_in[:, n // HALVES, n % HALVES, :], gate_w_sb[:, n, :], n == 0, False)
            mm(spare[0:B, 0:E], ones[0:1, 0:B], gate_b_sb[0:1, :], False, True)
            for n in range(HALVES):
                mm(bulk[1][0:B, 0:2 * E], silu[:, n * B:(n + 1) * B], time_w_sb[:, n, :], n == 0, False)
            mm(bulk[1][0:B, 0:2 * E], ones[0:1, 0:B], time_b_sb[0:1, :], False, True).then_inc(g_pe, 1)
            pe.wait_ge(g_dve, 2)
            mm(spare[:, 0:E * B], ones[0:B, :], spread[:].rearrange("p e b -> p (e b)"), True, True).then_inc(g_pe, 1)

            XB = BLOCKS + 1
            pe.wait_ge(wx_in, 32)
            pe.wait_ge(x2_sum, E)
            for fill in range(FILLS):
                if fill >= 2:
                    pe.wait_ge(xz_ready, FILLS * XB + fill - 1)
                for r in range(2 * HALVES):
                    x_product(fill, r, x2[:, 0])
            pe.wait_ge(wh_split, 2)

            def out_transposes(n):
                pe.wait_ge(x3_ready, n + 1)
                for j in range(XTILES):
                    for k in range(HALVES):
                        half = B // XTILES
                        last = nc.tensor.transpose(
                            bulk[0][:, j * D + k * P:j * D + (k + 1) * P],
                            x3[:, k, half * j:half * (j + 1)].rearrange("p b t -> p (b t)"), ident[:])
                last.then_inc(out_ps, 1)

            def body_b(i, first, last):
                for s in range(PASS):
                    slot, parity = s % BLOCK, s // BLOCK
                    n = 2 * i + parity + 1
                    lstm_step(T + PASS * i + s, 2)
                    if slot == 0:
                        pe.wait_ge(xz_ready, FILLS * (XB + n))
                    if slot == 1 and not (first and parity == 0):
                        out_transposes(n - 2)
                    if not (last and parity == 1):
                        if slot == 5:
                            pe.wait_ge(x2_sum, E * (n + 1))
                            if not (first and parity == 0):
                                pe.wait_ge(out_ready, n - 1)
                        next_products(XB + n, slot, x2[:, 1 - parity], None)
                    if experts_b(i, s) is not None:
                        expert_products(*experts_b(i, s))

            body_b(0, True, False)
            with pe.Fori(1, PASSES - 1) as i:
                body_b(i, False, False)
            body_b(PASSES - 1, False, True)
            out_transposes(BLOCKS - 1)

        @block.scalar
        def _(act):
            def lstm_gates(step):
                act.wait_ge(zs_ready, step + 1)
                nc.scalar.activation(gc[:, :, 0], zs[:, :, 0], ACT.Tanh).then_inc(gates_ready, 1)
                nc.scalar.activation(sig[:].rearrange("p h g b -> p h (g b)"),
                                     zs[:, :, 1:GATES].rearrange("p h g b -> p h (g b)"),
                                     ACT.Sigmoid).then_inc(gates_ready, 1)

            def lstm_cell(step):
                act.wait_ge(cell_ready, step + 1)
                nc.scalar.activation(tanh_c[:], gc[:, :, 1], ACT.Tanh).then_inc(cell_tanh, 1)

            def rnn_step(slot, parity, done, c):
                act.wait_ge(rnn_zs_ready, done + 1)
                nc.scalar.activation(rnn_h[:, parity, slot], rnn_zs[:], ACT.Tanh).then_inc(rnn_tanh, 1)

            def expert_steps(win, w, c):
                for q in range(GROUPS):
                    if w == win.tanh[q]:
                        act.wait_ge(poly_done, GROUPS * c + q + 1)
                        nc.scalar.activation(inner[:, q % 2], inner[:, q % 2], ACT.Tanh,
                                             scale=TANH_SCALE).then_inc(th_done, 1)
                for e in range(NE):
                    if w == win.out[e]:
                        act.wait_ge(down_done, NE * c + e + 1)
                        act.wait_ge(expert_dma[e], 32 + 16 * c)
                        for m in range(HALVES):
                            bias = column("eb2", HALVES * e + m) if e < E else column("sb2", m)
                            nc.scalar.activation(y[:, e, :, m, :],
                                                 down_ps[:, m * TOK:(m + 1) * TOK].rearrange("p (t b) -> p t b", b=B),
                                                 ACT.Identity, bias=bias, scale=0.5).then_inc(y_evac, 1)
                for q in range(GROUPS):
                    if w == win.square[q]:
                        act.wait_ge(u_ready, GROUPS * c + q + 1)
                        if q >= 2:
                            act.wait_ge(hid_ready, GROUPS * c + q - 1)
                        nc.scalar.activation(inner[:, q % 2], u[:, q % 4], ACT.Square,
                                             scale=CUBIC ** 0.5).then_inc(sq_ready, 1)

            act.wait_ge(vec_ready, 1)
            nc.scalar.activation(silu[:], columns("cond", COLS), ACT.Sigmoid).then_inc(g_act, 1)

            def body_a(i):
                for s in range(PASS if lstm_at(i) else BLOCK):
                    if lstm_at(i):
                        lstm_gates(PASS * i + s)
                    r = rnn_at(i, s)
                    if r is not None:
                        rnn_step(*r)
                    if lstm_at(i):
                        lstm_cell(PASS * i + s)
                    if experts_a(i, s) is not None:
                        expert_steps(*experts_a(i, s))

            body_a(0)
            with act.Fori(1, PASSES) as i:
                body_a(i)
            body_a(PASSES)

            act.wait_ge(g_shifted, 1)
            nc.scalar.activation(gs[:, 12:16], gs[:, 8:12], ACT.Exp).then_inc(g_act, 1)

            def body_b(i):
                for s in range(PASS):
                    lstm_gates(T + PASS * i + s)
                    lstm_cell(T + PASS * i + s)
                    if experts_b(i, s) is not None:
                        expert_steps(*experts_b(i, s))

            body_b(0)
            with act.Fori(1, PASSES - 1) as i:
                body_b(i)
            body_b(PASSES - 1)

        @block.vector
        def _(dve):
            chained = [0]

            def then(ins):
                chained[0] += 1
                ins.then_inc(g_chain, 1)
                dve.wait_ge(g_chain, chained[0])

            def find_max(n, w):
                nc.vector.tensor_reduce(w_max[:, n:n + 1], w[:].rearrange("p k n -> p (k n)"), AX_X, ALU.max,
                                        apply_absolute_value=True).then_inc(w_max_ready, 1)

            def split_weights(n, w, w16, done):
                one = slice(n, n + 1)
                dve.wait_ge(w_top_ready, n + 1)
                then(nc.vector.tensor_scalar(w_pow[:, one], w_top[:, one], 2.0 ** -100, None, ALU.max))
                then(nc.vector.tensor_scalar(w_pow[:, one].bitcast(I32), w_pow[:, one].bitcast(I32), 0x7F800000, None,
                                             ALU.bitwise_and))
                then(nc.vector.reciprocal(w_inv[:, one], w_pow[:, one]))
                then(nc.vector.tensor_scalar(up_scale[:, one], w_inv[:, one], W_TOP, None, ALU.mult))
                nc.vector.tensor_scalar(unscale[:, one], w_pow[:, one], 1.0 / (W_TOP * H_SCALE), None, ALU.mult)
                then(nc.vector.tensor_scalar(w16[:, 0], w[:], up_scale[:, one], None, ALU.mult))
                nc.vector.scalar_tensor_tensor(w16[:, 1], w[:], up_scale[:, one], w16[:, 0], ALU.mult,
                                               ALU.subtract).then_inc(done, 1)

            def start_lstm():
                nc.vector.memset(gc[:, :, 1], 0.0)
                nc.vector.memset(h16[:], 0.0).then_inc(h_ready, 1)

            def add_first_h(n):
                dve.wait_ge(h0_z, n)
                dve.wait_ge(xz_ready, FILLS * (1 if n == 1 else BLOCKS + 2))
                nc.vector.tensor_tensor(xz[:, 0, 0].rearrange("p h g b -> p (h g b)"),
                                        xz[:, 0, 0].rearrange("p h g b -> p (h g b)"),
                                        spare[:, 0:GATES * COLS], ALU.add).then_inc(h0_added, 1)

            def lstm_z(step, n, parity, slot):
                zp = z[:, 0:GATES * COLS * PARTS].rearrange("p (n a b) -> p n a b", a=PARTS, b=B)
                flat = "p h g b -> p (h g) b"
                dve.wait_ge(z_ready, step + 1)
                nc.vector.scalar_tensor_tensor(zt[:].rearrange(flat), zp[:, :, 1], unscale[:, n:n + 1],
                                               xz[:, parity, slot].rearrange(flat), ALU.mult,
                                               ALU.add).then_inc(zt_ready, 1)
                dve.wait_ge(zt_ready, step + 1)
                nc.vector.scalar_tensor_tensor(zs[:].rearrange(flat), zp[:, :, 0], unscale[:, n:n + 1],
                                               zt[:].rearrange(flat), ALU.mult, ALU.add).then_inc(zs_ready, 1)

            def lstm_c(step):
                dve.wait_ge(gates_ready, 2 * (step + 1))
                nc.vector.tensor_tensor(prod[:], sig[:, :, 0:2], gc[:], ALU.mult).then_inc(prod_ready, 1)
                dve.wait_ge(prod_ready, step + 1)
                nc.vector.tensor_tensor(gc[:, :, 1], prod[:, :, 0], prod[:, :, 1], ALU.add).then_inc(cell_ready, 1)

            def lstm_h(step, slot):
                dve.wait_ge(cell_tanh, step + 1)
                nc.vector.tensor_tensor(h_seq[:, slot], sig[:, :, 2], tanh_c[:], ALU.mult).then_inc(full_ready, 1)
                nc.vector.scalar_tensor_tensor(h16[:, :, 0], sig[:, :, 2], H_SCALE, tanh_c[:], ALU.mult,
                                               ALU.mult).then_inc(h1_ready, 1)
                dve.wait_ge(full_ready, step + 1)
                dve.wait_ge(h1_ready, step + 1)
                nc.vector.scalar_tensor_tensor(h16[:, :, 1], h_seq[:, slot], H_SCALE, h16[:, :, 0], ALU.mult,
                                               ALU.subtract).then_inc(h_ready, 1)

            def rnn_z(slot, parity, done, c):
                if slot == 0:
                    dve.wait_ge(rnn_xz_ps, c + 1)
                    for m in range(HALVES):
                        last = nc.vector.tensor_scalar(
                            rnn_xz[:, :, m, :], bulk[1][:, m * TOK:(m + 1) * TOK].rearrange("p (t b) -> p t b", b=B),
                            column("L1_b", m), None, ALU.add)
                    last.then_inc(rnn_xz_ready, 1)
                    dve.wait_ge(rnn_xz_ready, c + 1)
                    if isinstance(c, int) and c == 0:
                        then(nc.vector.tensor_tensor(rnn_xz[:, 0].rearrange("p h b -> p (h b)"),
                                                     rnn_xz[:, 0].rearrange("p h b -> p (h b)"), first_rnn[:],
                                                     ALU.add))
                zp = z1[:, 0:COLS * PARTS].rearrange("p (n a b) -> p n a b", a=PARTS, b=B)
                dve.wait_ge(rnn_z_ready, done + 2)
                nc.vector.scalar_tensor_tensor(rnn_zt[:], zp[:, :, 1], unscale[:, 1:2], rnn_xz[:, slot], ALU.mult,
                                               ALU.add).then_inc(rnn_zt_ready, 1)
                dve.wait_ge(rnn_zt_ready, done + 1)
                nc.vector.scalar_tensor_tensor(rnn_zs[:], zp[:, :, 0], unscale[:, 1:2], rnn_zt[:], ALU.mult,
                                               ALU.add).then_inc(rnn_zs_ready, 1)

            def rnn_split(slot, parity, done, c):
                dve.wait_ge(rnn_tanh, done + 1)
                h = rnn_h[:, parity, slot]
                nc.vector.tensor_scalar(rnn_h16[:, :, 0], h, H_SCALE, None, ALU.mult).then_inc(rnn_h1_ready, 1)
                dve.wait_ge(rnn_h1_ready, done + 1)
                nc.vector.scalar_tensor_tensor(rnn_h16[:, :, 1], h, H_SCALE, rnn_h16[:, :, 0], ALU.mult,
                                               ALU.subtract).then_inc(rnn_h_ready, 1)

            def take_xT(n, parity):
                dve.wait_ge(xT_ps, n + 1)
                for k in range(HALVES):
                    last = nc.vector.tensor_copy(
                        xT[:, parity, :, k, :].rearrange("p t b -> p b t"),
                        bulk[0][:, k * TOK:(k + 1) * TOK].rearrange("p (b t) -> p b t", t=BLOCK))
                last.then_inc(xT_ready, 1)

            def take_xz(n, fill, parity, bias):
                m, gate = fill // 2, 2 * (fill % 2)
                dve.wait_ge(xz_ps, FILLS * n + fill + 1)
                for j in range(2):
                    last = nc.vector.tensor_scalar(
                        xz[:, parity, :, m, gate + j, :],
                        bulk[fill % 2][:, j * TOK:(j + 1) * TOK].rearrange("p (t b) -> p t b", b=B),
                        column(bias, GATES * m + gate + j), None, ALU.add)
                last.then_inc(xz_ready, 1)

            def next_products(n, slot, parity, bias):
                fill, r = divmod(slot - 5, 6)
                if 0 <= fill < FILLS and r == 4:
                    take_xz(n, fill, parity, bias)

            def expert_steps(win, w, c):
                for q in range(GROUPS):
                    if w == win.hid[q]:
                        dve.wait_ge(th_done, GROUPS * c + q + 1)
                        nc.vector.scalar_tensor_tensor(hid[:, q % 4], inner[:, q % 2], 1.0, u[:, q % 4],
                                                       ALU.add, ALU.mult).then_inc(hid_ready, 1)
                for q in range(GROUPS):
                    if w == win.up[q]:
                        dve.wait_ge(up_done, GROUPS * c + q + 1)
                        e, g = q // GPE, q % GPE
                        bias = bias_over("eb1", GROUP, e * TILES + g * GROUP) if e < E else \
                            bias_over("sb1", GROUP, g * GROUP)
                        nc.vector.tensor_tensor(u[:, q % 4].rearrange("p (j n) -> p j n", j=GROUP),
                                                up_ps[q % 2][:].rearrange("p (j n) -> p j n", j=GROUP),
                                                bias, ALU.add).then_inc(u_ready, 1)

            dve.wait_ge(wh_in, 16)
            find_max(0, wh)
            dve.wait_ge(vec_ps, 1)
            nc.vector.tensor_copy(vec[:, 0:NROWS], up_ps[0][:, 0:NROWS]).then_inc(vec_ready, 1)
            take_xT(0, 0)
            dve.wait_ge(w1_in, 32)
            find_max(1, wh1)
            split_weights(0, wh, wh16, wh_split)
            dve.wait_ge(vec_ready, 1)
            for fill in range(FILLS):
                take_xz(0, fill, 0, "L0_b")
            add_first_h(1)
            start_lstm()
            split_weights(1, wh1, wh1_16, wh1_split)
            dve.wait_ge(rnn_z_ready, 1)
            nc.vector.tensor_copy(first_rnn[:], z1[:, 0:COLS]).then_inc(first_rnn_ready, 1)
            nc.vector.memset(rnn_h16[:], 0.0).then_inc(rnn_h_ready, 1)
            dve.wait_ge(h0_added, 1)

            def body_a(i):
                for s in range(PASS if lstm_at(i) else BLOCK):
                    slot, parity = s % BLOCK, s // BLOCK
                    step = PASS * i + s
                    r = rnn_at(i, s)
                    if lstm_at(i):
                        lstm_z(step, 0, parity, slot)
                    if r is not None:
                        rnn_z(*r)
                    if lstm_at(i):
                        lstm_c(step)
                    if r is not None:
                        rnn_split(*r)
                    if lstm_at(i):
                        lstm_h(step, slot)
                        n = 2 * i + parity + 1
                        if slot == 3:
                            take_xT(n, 1 - parity)
                        next_products(n, slot, 1 - parity, "L0_b")
                        if slot == BLOCK - 1:
                            dve.wait_ge(full_ready, step + 1)
                            nc.vector.tensor_tensor(rnn_x[:, parity], xT[:, parity], h_seq[:],
                                                    ALU.add).then_inc(rnn_x_ready, 1)
                    if r is not None and r[0] == BLOCK - 1:
                        _, rparity, done, c = r
                        dve.wait_ge(rnn_tanh, done + 1)
                        nc.vector.tensor_tensor(x1[:, bass.ds(c * BLOCK, BLOCK)].rearrange("p t h b -> p (t h b)"),
                                                rnn_x[:, rparity].rearrange("p t h b -> p (t h b)"),
                                                rnn_h[:, rparity].rearrange("p t h b -> p (t h b)"),
                                                ALU.add).then_inc(x1_ready, 1)
                    if experts_a(i, s) is not None:
                        expert_steps(*experts_a(i, s))

            body_a(0)
            with dve.Fori(1, PASSES) as i:
                body_a(i)
            dve.wait_ge(wh_in, 32)
            find_max(2, wh)
            split_weights(2, wh, wh16, wh_split)
            dve.wait_ge(h0_z, 2)
            nc.vector.tensor_copy(first_h3[:], spare[:, 0:GATES * COLS]).then_inc(h0_added, 1)
            body_a(PASSES)

            dve.wait_ge(x1_ready, BLOCKS)
            for n, (a, b_) in enumerate(SPANS):
                last = nc.vector.reduce_sum(sums[:, n].rearrange("p h b -> p (h b)"),
                                            x1[:, a:b_].rearrange("p t h b -> p (h b) t"), AX_X)
            then(last)
            head, wrist, proprio = (sums[:, n] for n in range(3))
            lengths = [b_ - a for a, b_ in SPANS]
            then(nc.vector.tensor_tensor(gate_in[:, 1], head, proprio, ALU.add))
            then(nc.vector.tensor_tensor(gate_in[:, 2], wrist, proprio, ALU.add))
            then(nc.vector.tensor_tensor(gate_in[:, 0], gate_in[:, 1], wrist, ALU.add))
            then(nc.vector.tensor_scalar(gate_in[:, 0], gate_in[:, 0], 1.0 / T, None, ALU.mult))
            then(nc.vector.tensor_scalar(gate_in[:, 1], gate_in[:, 1], 1.0 / (lengths[0] + lengths[2]), None, ALU.mult))
            then(nc.vector.tensor_scalar(gate_in[:, 2], gate_in[:, 2], 1.0 / (lengths[1] + lengths[2]), None, ALU.mult))
            dve.wait_ge(g_act, 1)
            then(nc.vector.tensor_tensor(gtmp[:], silu[:], columns("cond", COLS), ALU.mult))
            nc.vector.tensor_copy(silu[:].rearrange("p (h b) -> p h b", h=HALVES),
                                  gtmp[:].rearrange("p (b h) -> p h b", h=HALVES)).then_inc(g_dve, 1)
            dve.wait_ge(g_pe, 1)
            mod, logits, shifted, expd = gs[:, 0:8], gs[:, 16:20], gs[:, 8:12], gs[:, 12:16]
            score, rank, top, wgt = gs[:, 20:24], gs[:, 24:28], gs[:, 28:32], gs[:, 32:36]
            one = gs[:, 40:41]
            then(nc.vector.tensor_copy(mod, bulk[1][0:B, 0:2 * E]))
            then(nc.vector.tensor_scalar(mod[:, 0:E], mod[:, 0:E], 1.0, None, ALU.add))
            then(nc.vector.tensor_tensor(logits, spare[0:B, 0:E], mod[:, 0:E], ALU.mult))
            then(nc.vector.tensor_tensor(logits, logits, mod[:, E:2 * E], ALU.add))
            then(nc.vector.reduce_max(one, logits, AX_X))
            nc.vector.tensor_scalar(shifted, logits, one, None, ALU.subtract).then_inc(g_shifted, 1)
            dve.wait_ge(g_act, 2)
            then(nc.vector.reduce_sum(gs[:, 41:42], expd, AX_X))
            then(nc.vector.reciprocal(gs[:, 42:43], gs[:, 41:42]))
            then(nc.vector.tensor_scalar(score, expd, gs[:, 42:43], None, ALU.mult))
            then(nc.vector.memset(rank, 0.0))
            for j in range(E):
                s_j = score[:, j:j + 1]
                if j > 0:
                    then(nc.vector.scalar_tensor_tensor(rank[:, 0:j], score[:, 0:j], s_j, rank[:, 0:j],
                                                        ALU.is_lt, ALU.add))
                if j < E - 1:
                    then(nc.vector.scalar_tensor_tensor(rank[:, j + 1:E], score[:, j + 1:E], s_j, rank[:, j + 1:E],
                                                        ALU.is_le, ALU.add))
            then(nc.vector.scalar_tensor_tensor(top, rank, 2.0, score, ALU.is_lt, ALU.mult))
            then(nc.vector.reduce_sum(gs[:, 43:44], top, AX_X))
            then(nc.vector.tensor_scalar(gs[:, 44:45], gs[:, 43:44], 1e-8, None, ALU.add))
            then(nc.vector.reciprocal(gs[:, 45:46], gs[:, 44:45]))
            then(nc.vector.tensor_scalar(wgt, top, gs[:, 45:46], None, ALU.mult))
            nc.vector.tensor_tensor(spread[:], wgt[:, :, None].to_broadcast([B, E, B]),
                                    ident[0:B, None, 0:B].to_broadcast([B, E, B]), ALU.mult).then_inc(g_dve, 1)
            dve.wait_ge(g_pe, 2)
            nc.vector.tensor_copy(wb[:].rearrange("p e b -> p (e b)"), spare[:, 0:E * B]).then_inc(wb_ready, 1)

            XB = BLOCKS + 1
            for fill in range(FILLS):
                take_xz(XB, fill, 0, "L3_b")
            dve.wait_ge(xz_ready, FILLS * (XB + 1))
            dve.wait_ge(h0_added, 2)
            nc.vector.tensor_tensor(xz[:, 0, 0].rearrange("p h g b -> p (h g b)"),
                                    xz[:, 0, 0].rearrange("p h g b -> p (h g b)"), first_h3[:],
                                    ALU.add).then_inc(h0_added, 1)
            dve.wait_ge(h0_added, 3)
            start_lstm()

            def body_b(i, first, last_pass):
                for s in range(PASS):
                    slot, parity = s % BLOCK, s // BLOCK
                    n = 2 * i + parity + 1
                    step = T + PASS * i + s
                    lstm_z(step, 2, parity, slot)
                    lstm_c(step)
                    lstm_h(step, slot)
                    if slot == 2 and not (first and parity == 0):
                        take_out(n - 2)
                    if not (last_pass and parity == 1):
                        next_products(XB + n, slot, 1 - parity, "L3_b")
                    if slot == BLOCK - 1:
                        dve.wait_ge(full_ready, step + 1)
                        for m in range(HALVES):
                            last = nc.vector.tensor_tensor(x3[:, m], x2[:, parity, :, m, :].rearrange("p t b -> p b t"),
                                                           h_seq[:, :, m, :].rearrange("p t b -> p b t"), ALU.add)
                        last.then_inc(x3_ready, 1)
                    if experts_b(i, s) is not None:
                        expert_steps(*experts_b(i, s))

            def take_out(n):
                dve.wait_ge(out_ps, n + 1)
                if not (isinstance(n, int) and n == 0):
                    dve.wait_ge(stored, 16 * XTILES * n)
                nc.vector.tensor_copy(out_rows[:].rearrange("p j d -> p (j d)"), bulk[0][:]).then_inc(out_ready, 1)

            body_b(0, True, False)
            with dve.Fori(1, PASSES - 1) as i:
                body_b(i, False, False)
            body_b(PASSES - 1, False, True)
            take_out(BLOCKS - 1)

        @block.gpsimd
        def _(pool):
            nc.gpsimd.memset(ident[:], 0.0).then_inc(pool_c, 1)
            nc.gpsimd.memset(ones[:], 1.0).then_inc(consts, 1)
            pool.wait_ge(pool_c, 1)
            nc.gpsimd.affine_select(out=ident[:], in_=ident[:], compare_op=ALU.not_equal, fill=1.0, base=0,
                                    pattern=[[-1, P]], channel_multiplier=1).then_inc(consts, 1)
            nc.gpsimd.memset(keep[:], 1.0).then_inc(pool_c, 1)
            pool.wait_ge(pool_c, 2)
            nc.gpsimd.memset(keep[:, 0, THIRD:2 * THIRD], 0.0).then_inc(pool_c, 1)
            nc.gpsimd.memset(keep[:, 1, 0:THIRD], 0.0).then_inc(pool_c, 1)
            pool.wait_ge(pool_c, 4)

            def spread_max(n):
                pool.wait_ge(w_max_ready, n + 1)
                nc.gpsimd.partition_all_reduce(w_top[:, n:n + 1], w_max[:, n:n + 1], P,
                                               bass.bass_isa.ReduceOp.max).then_inc(w_top_ready, 1)

            spread_max(0)
            spread_max(1)

            def expert_steps(win, w, c):
                for q in range(GROUPS):
                    if w == win.square[q]:
                        n = GROUPS * c + q
                        pool.wait_ge(sq_ready, n + 1)
                        v = inner[:, q % 2]
                        nc.gpsimd.tensor_tensor(v, v, u[:, q % 4], ALU.mult).then_inc(pool_chain, 1)
                        pool.wait_ge(pool_chain, n + 1)
                        nc.gpsimd.tensor_tensor(v, v, u[:, q % 4], ALU.add).then_inc(poly_done, 1)
                for e in (1, 2, E):
                    if w == win.out[e]:
                        pool.wait_ge(y_evac, 2 * (NE * c + e + 1))
                        if e < E:
                            mask = keep[:, e - 1, bass.ds(c * BLOCK, BLOCK)]
                            nc.gpsimd.tensor_tensor(
                                y[:, e].rearrange("p t h b -> p t (h b)"), y[:, e].rearrange("p t h b -> p t (h b)"),
                                mask[:, :, None].to_broadcast([P, BLOCK, COLS]), ALU.mult).then_inc(y_masked, 1)
                        else:
                            nc.gpsimd.tensor_tensor(
                                y[:, e].rearrange("p t h b -> p (t h b)"), y[:, e].rearrange("p t h b -> p (t h b)"),
                                x1[:, bass.ds(c * BLOCK, BLOCK)].rearrange("p t h b -> p (t h b)"),
                                ALU.add).then_inc(y_shared, 1)

            def body_a(i):
                for s in range(PASS if lstm_at(i) else BLOCK):
                    if experts_a(i, s) is not None:
                        expert_steps(*experts_a(i, s))

            body_a(0)
            with pool.Fori(1, PASSES) as i:
                body_a(i)
            spread_max(2)
            body_a(PASSES)

            def combine(n, parity, k):
                flat = "p t h b -> p (t h) b"
                acc = x2[:, parity].rearrange(flat)
                back = y_back[:, k % 2].rearrange(flat)
                per = (NE + 1 - k % 2) // 2
                pool.wait_ge(y_loaded[k % 2], 16 * (per * n + k // 2 + 1))
                nc.gpsimd.tensor_tensor(part[:].rearrange(flat), back,
                                        wb[:, k - 1, None, :].to_broadcast([P, 2 * BLOCK, B]),
                                        ALU.mult).then_inc(x2_part, 1)
                if k == 1:
                    base = y_back[:, 0].rearrange(flat)
                    pool.wait_ge(y_loaded[0], 16 * ((NE + 1) // 2 * n + 1))
                else:
                    base = acc
                    pool.wait_ge(x2_sum, E * n + k - 1)
                pool.wait_ge(x2_part, E * n + k)
                nc.gpsimd.tensor_tensor(acc, base, part[:].rearrange(flat), ALU.add).then_inc(x2_sum, 1)

            pool.wait_ge(wb_ready, 1)
            for k in range(1, NE):
                combine(0, 0, k)

            def body_b(i, first, last):
                for s in range(PASS):
                    parity = s // BLOCK
                    n = 2 * i + parity + 1
                    if 1 <= s % BLOCK < NE and not (last and parity == 1):
                        if s % BLOCK == 1 and not (first and parity == 0):
                            pool.wait_ge(x3_ready, n - 1)
                        combine(n, 1 - parity, s % BLOCK)
                    if experts_b(i, s) is not None:
                        expert_steps(*experts_b(i, s))

            body_b(0, True, False)
            with pool.Fori(1, PASSES - 1) as i:
                body_b(i, False, False)
            body_b(PASSES - 1, False, True)


_INS = ["x", "cond_1024", "L0_cond_Wx", "L0_cond_Wh", "L0_cond_b", "L1_cond_Wx", "L1_cond_Wh", "L1_cond_b",
        "L2_cond_gate_w", "L2_cond_gate_b", "L2_cond_time_w", "L2_cond_time_b", "L2_cond_ew1", "L2_cond_eb1",
        "L2_cond_ew2", "L2_cond_eb2", "L2_cond_sw1", "L2_cond_sb1", "L2_cond_sw2", "L2_cond_sb2",
        "L3_cond_Wx", "L3_cond_Wh", "L3_cond_b"]


def kernel(**inputs):
    import numpy as _np
    import concourse.bacc as _bacc
    from concourse import mybir as _mybir
    from concourse.bass_utils import run_bass_kernel_spmd as _run

    nc = _bacc.Bacc("TRN2", target_bir_lowering=False, num_devices=1)
    arrays, args = {}, []
    for name in _INS:
        a = _np.ascontiguousarray(inputs[name])
        arrays[f"in_{name}_dram"] = a
        args.append(nc.dram_tensor(f"in_{name}_dram", a.shape, _mybir.dt.from_np(a.dtype), kind="ExternalInput").ap())
    out = nc.dram_tensor("out_dram", (8, 256, 256), _mybir.dt.float32, kind="ExternalOutput").ap()
    cond_residual_kernel(nc, *args, out)
    r = _run(nc, [arrays], core_ids=[0])
    return r.results[0]["out_dram"]
```

```python
from contextlib import ExitStack

import concourse.bass as bass
from concourse import mybir

F32 = mybir.dt.float32
F16 = mybir.dt.float16
I32 = mybir.dt.int32
ALU = mybir.AluOpType
ACT = mybir.ActivationFunctionType
AX_X = mybir.AxisListType.X

P = 128
HALVES = 2
GATES = 4
PARTS = 2
GATE_COLUMN = (3, 1, 0, 2)
CANDIDATE = 3
BLOCK = 32
PASS = 2 * BLOCK
RNN_LAG = BLOCK + 1
EXPERTS_FROM = 1
GROUP = 2
SPREAD = 46
PRODUCTS_SLOT = 9
TANH_SCALE = 0.7978845608028654
CUBIC = 0.044715
H_SCALE = 256.0
W_TOP = 2.0 ** 14
W_LEAST = 2.0 ** -40


def cond_residual_kernel(nc, x, cond_1024, L0_Wx, L0_Wh, L0_b, L1_Wx, L1_Wh, L1_b, gate_w, gate_b, time_w, time_b,
                         ew1, eb1, ew2, eb2, sw1, sb1, sw2, sb2, L3_Wx, L3_Wh, L3_b, out):
    B, T, D = x.shape
    E, _, H = ew1.shape
    assert D == HALVES * P and B == 8 and T % PASS == 0 and L0_Wh.shape == (D, GATES * D)
    PASSES = T // PASS
    BLOCKS = T // BLOCK
    TOK = BLOCK * B
    COLS = HALVES * B
    NE = E + 1
    TILES = H // P
    GPE = TILES // GROUP
    GROUPS = NE * GPE
    THIRD = T // 3
    SPANS = ((0, THIRD), (THIRD, 2 * THIRD), (2 * THIRD, T))
    FILLS = HALVES * GATES // 2
    BANK = 2 * TOK
    assert BANK == 512 and GROUP * TOK == BANK and HALVES * TOK == BANK
    XTILES = TOK // P

    LAID = 8

    def x_product_at(slot):
        fill, r = divmod(slot - PRODUCTS_SLOT, 5)
        return (fill, r) if 0 <= fill < FILLS and r < 2 * HALVES else None

    LAG = 3
    items = []
    for q in range(GROUPS + LAG):
        if q < GROUPS:
            items.append(("up", q))
        if q >= LAG:
            items.append(("down", q - LAG))
    MM_PER_ITEM = GROUP * HALVES
    MMS = len(items) * MM_PER_ITEM

    class Window:

        def __init__(self, others, delay):
            share = 0
            while sum(max(share - used, 0) for used in others) < MMS:
                share += 1 / 64
            room, self.step_of = 0, []
            for w, used in enumerate(others):
                room += max(share - used, 0)
                while len(self.step_of) < min(int(room + 1e-6), MMS):
                    self.step_of.append(w)
            self.step_of += [len(others) - 1] * (MMS - len(self.step_of))
            begin = {it: self.step_of[n * MM_PER_ITEM] for n, it in enumerate(items)}
            end = {it: self.step_of[(n + 1) * MM_PER_ITEM - 1] for n, it in enumerate(items)}
            self.up = [end["up", q] for q in range(GROUPS)]
            self.square = [step + delay for step in self.up]
            self.tanh = self.hid = [min([self.square[q] + 2, begin["down", q] - 1] + self.square[q + 2:q + 3])
                                    for q in range(GROUPS)]
            assert all(self.square[q] < self.hid[q] for q in range(GROUPS))
            assert all(self.hid[q] < begin["down", q] for q in range(GROUPS))
            assert all(self.hid[q] <= self.square[q + 2] for q in range(GROUPS - 2))
            assert all(self.hid[q] <= self.up[q + 4] for q in range(GROUPS - 4))
            self.out = [end["down", GPE * (e + 1) - 1] for e in range(NE)]

        def matmuls(self, w):
            return [n for n in range(MMS) if self.step_of[n] == w]

    def others_a(s):
        slot = s % BLOCK
        return (x_product_at(slot) is not None) + 2 * (slot % LAID == LAID - 1) + 2 * (slot == 2) + 4 * (slot == 0)

    def others_b(s):
        slot = s % BLOCK
        return (x_product_at(slot) is not None) + 2 * (slot % LAID == LAID - 1) + (slot == 1)

    SLOW = Window([others_a(s) for s in range(EXPERTS_FROM, PASS)], 1)
    FAST = Window([0] * (RNN_LAG - EXPERTS_FROM), 0)
    IN_B = [Window([others_b(s) for s in range(SPREAD * c, SPREAD * (c + 1))], 1) for c in range(BLOCKS - PASSES)]

    ROWS = {}
    at = 0
    for name, rows_ in (("eb1", E * TILES), ("sb1", TILES), ("eb2", E * HALVES), ("sb2", HALVES),
                        ("L0_b", GATES * HALVES), ("L1_b", HALVES), ("L3_b", GATES * HALVES), ("cond", B * HALVES)):
        ROWS[name] = at
        at += rows_
    NROWS = at

    with ExitStack() as ctx:
        def sb(name, shape, dt=F32):
            return ctx.enter_context(nc.sbuf_tensor(name, shape, dt))

        def psum(name):
            return ctx.enter_context(nc.psum_tensor(name, [P, 512], F32))

        def sem(name):
            return ctx.enter_context(nc.semaphore(name))

        wx = sb("wx", [P, HALVES, GATES * D])
        wh = sb("wh", [P, HALVES, GATES * D])
        wh16 = sb("wh16", [P, PARTS, HALVES, GATES * D], F16)
        wx1 = sb("wx1", [P, HALVES, D])
        wh1 = sb("wh1", [P, HALVES, D])
        wh1_16 = sb("wh1_16", [P, PARTS, HALVES, D], F16)
        up_w = sb("up_w", [P, NE, HALVES, H])
        down_w = sb("down_w", [P, NE, TILES, D])
        rows = sb("rows", [P, P])
        vec = sb("vec", [P, P])
        gate_w_sb = sb("gate_w_sb", [P, 3 * HALVES, E])
        time_w_sb = sb("time_w_sb", [P, HALVES, 2 * E])
        gate_b_sb = sb("gate_b_sb", [1, E])
        time_b_sb = sb("time_b_sb", [1, 2 * E])
        ident = sb("ident", [P, P])
        ones = sb("ones", [P, P])
        keep = sb("keep", [P, 2, T])
        w_max = sb("w_max", [P, 3])
        w_top = sb("w_top", [P, 3])
        w_pow = sb("w_pow", [P, 3])
        w_inv = sb("w_inv", [P, 3])
        up_scale = sb("up_scale", [P, 3])
        up_half = sb("up_half", [P, 3])
        z_scale = sb("z_scale", [P, 3])
        ident_z = sb("ident_z", [P, 2, P])
        unscale = sb("unscale", [P, 3])
        x_rows = sb("x_rows", [P, XTILES, D])
        xT = sb("xT", [P, 2, BLOCK, HALVES, B])
        xz = sb("xz", [P, 2, HALVES, BLOCK, GATES, B])
        h_seq = sb("h_seq", [P, BLOCK, HALVES, B])
        h16 = sb("h16", [P, HALVES, PARTS, B], F16)
        zs = sb("zs", [P, HALVES, GATES, B])
        cell = sb("cell", [P, HALVES, 1 + GATES, B])
        prod = sb("prod", [P, HALVES, 2, B])
        o_scaled = sb("o_scaled", [P, HALVES, B])
        tanh_c = sb("tanh_c", [P, HALVES, B])
        rnn_x = sb("rnn_x", [P, 2, BLOCK, HALVES, B])
        rnn_xz = sb("rnn_xz", [P, BLOCK, HALVES, B])
        rnn_h = sb("rnn_h", [P, 2, BLOCK, HALVES, B])
        rnn_h16 = sb("rnn_h16", [P, HALVES, PARTS, B], F16)
        first_rnn = sb("first_rnn", [P, COLS])
        first_h3 = sb("first_h3", [P, GATES * COLS])
        rnn_zt = sb("rnn_zt", [P, HALVES, B])
        rnn_zs = sb("rnn_zs", [P, HALVES, B])
        x1 = sb("x1", [P, T, HALVES, B])
        u = sb("u", [P, 4, BANK])
        inner = sb("inner", [P, 2, BANK])
        hid = sb("hid", [P, 4, BANK])
        y = sb("y", [P, NE, BLOCK, HALVES, B])
        sums = sb("sums", [P, 3, HALVES, B])
        gate_in = sb("gate_in", [P, 3, HALVES, B])
        gtmp = sb("gtmp", [P, COLS])
        silu = sb("silu", [P, COLS])
        gs = sb("gs", [B, 64])
        spread = sb("spread", [B, E, B])
        wb = sb("wb", [P, E, B])
        whf = wh[:].rearrange("p k n -> p (k n)")
        y_back = [whf[:, e * BANK:(e + 1) * BANK] for e in range(E)] + [wh1[:].rearrange("p k n -> p (k n)")]
        y_back = [a.rearrange("p (t h b) -> p t h b", h=HALVES, b=B) for a in y_back]
        x2 = rnn_x
        part = sb("part", [P, BLOCK, HALVES, B])
        x3 = sb("x3", [P, HALVES, B, BLOCK])
        out_rows = sb("out_rows", [P, XTILES, D])

        z_banks = [psum("z_half0"), psum("z_half1")]
        z1 = psum("z_rnn")
        up_ps = [psum("up0"), psum("up1")]
        down_ps = psum("down")
        bulk = [psum("bulk0"), psum("bulk1")]

        y_dram = nc.dram_tensor("expert_out", [BLOCKS, 1 + NE, P, BANK], F32, kind="Internal").ap()

        rows_in, x_in, wx_in, wh_in, w1_in, gate_params_in = (
            sem(n) for n in ("rows_in", "x_in", "wx_in", "wh_in", "w1_in", "gate_params_in"))
        expert_dma = [sem(f"expert_dma{e}") for e in range(NE)]
        consts, pool_c = sem("consts"), sem("pool_consts")
        vec_ps, vec_ready = sem("vec_ps"), sem("vec_ready")
        w_max_ready, w_top_ready, high_ready, wh_split, wh1_split = (
            sem(n) for n in ("w_max_ready", "w_top_ready", "high_ready", "wh_split", "wh1_split"))
        h0_z, h0_added, first_rnn_ready = sem("h0_z"), sem("h0_added"), sem("first_rnn_ready")
        xT_ps, xT_ready, xz_ps, xz_ready = sem("xT_ps"), sem("xT_ready"), sem("xz_ps"), sem("xz_ready")
        z_ready, zs_ready, gates_ready, prod_ready, cell_ready, o_ready, cell_tanh, h_parts, h_ready = (
            sem(n) for n in ("z_ready", "zs_ready", "gates_ready", "prod_ready", "cell_ready", "o_ready",
                             "cell_tanh", "h_parts", "h_ready"))
        rnn_x_ready, rnn_xz_ps, rnn_xz_ready = sem("rnn_x_ready"), sem("rnn_xz_ps"), sem("rnn_xz_ready")
        rnn_z_ready, rnn_zt_ready, rnn_zs_ready, rnn_tanh, rnn_h1_ready, rnn_h_ready = (
            sem(n) for n in ("rnn_z_ready", "rnn_zt_ready", "rnn_zs_ready", "rnn_tanh", "rnn_h1_ready", "rnn_h_ready"))
        x1_ready, up_done, u_ready, sq_ready, pool_chain, poly_done, th_done, hid_ready = (
            sem(n) for n in ("x1_ready", "up_done", "u_ready", "sq_ready", "pool_chain", "poly_done", "th_done",
                             "hid_ready"))
        down_done, y_evac, y_masked, y_shared = sem("down_done"), sem("y_evac"), sem("y_masked"), sem("y_shared")
        g_dve, g_act, g_pe, g_chain, g_shifted = (
            sem(n) for n in ("gate_dve", "gate_act", "gate_pe", "gate_chain", "gate_shifted"))
        wb_ready = sem("wb_ready")
        y_loaded = sem("y_loaded")
        x2_part, x2_sum = sem("x2_part"), sem("x2_sum")
        x3_ready, out_ps, out_ready, stored = sem("x3_ready"), sem("out_ps"), sem("out_ready"), sem("stored")

        block = ctx.enter_context(nc.Block())

        def column(name, n=0):
            return vec[:, ROWS[name] + n:ROWS[name] + n + 1]

        def columns(name, n, start=0):
            return vec[:, ROWS[name] + start:ROWS[name] + start + n]

        def cond_T():
            return columns("cond", COLS).rearrange("p (b h) -> p h b", h=HALVES)

        Z_COLS = GATES * PARTS * B
        assert LAID * Z_COLS == 512 and BLOCK % LAID == 0

        def z_of(slot, m):
            first = slot % LAID * Z_COLS
            return z_banks[m][:, first:first + Z_COLS].rearrange("p (g a b) -> p g a b", a=PARTS, b=B)

        def lstm_at(i):
            return not (isinstance(i, int) and i == PASSES)

        def rnn_at(i, s):
            if isinstance(i, int) and not 0 <= PASS * i + s - RNN_LAG < T:
                return None
            t = s - RNN_LAG
            return t % BLOCK, (t // BLOCK) % 2, i * PASS + t, 2 * i + t // BLOCK

        def rnn_products_at(i, s):
            if s % BLOCK != 0 or (isinstance(i, int) and i == s == 0) or (not lstm_at(i) and s > 0):
                return None
            return (s // BLOCK - 1) % 2, 2 * i + s // BLOCK - 1

        def experts_a(i, s):
            if (isinstance(i, int) and i == 0) or s < EXPERTS_FROM:
                return None
            if isinstance(i, int) and i == PASSES:
                return FAST, s - EXPERTS_FROM, PASSES - 1
            return SLOW, s - EXPERTS_FROM, i - 1

        FIRST_H3 = 20
        RNN_START = 2

        def experts_b(s):
            c = PASSES + s // SPREAD
            return (IN_B[c - PASSES], s % SPREAD, c) if c < BLOCKS else None

        LOAD_SLOT = 29
        assert all(SPREAD * (c - PASSES + 1) < BLOCK * (c - 2) + LOAD_SLOT for c in range(PASSES, BLOCKS))

        def combine(ops, on, n, parity, k):
            flat = "p t h b -> p (t h) b"
            acc = x2[:, parity].rearrange(flat)
            back = y_back[k - 1].rearrange(flat)
            if k == 1:
                on.wait_ge(y_loaded, 16 * NE * (n + 1))
                if n > 1:
                    on.wait_ge(x3_ready, n - 1)
            if n > 0 or k > 1:
                on.wait_ge(x2_sum, E * n + k - 1)
            ops.tensor_tensor(part[:].rearrange(flat), back, wb[:, k - 1, None, :].to_broadcast([P, 2 * BLOCK, B]),
                              ALU.mult).then_inc(x2_part, 1)
            on.wait_ge(x2_part, E * n + k)
            base = y_back[E].rearrange(flat) if k == 1 else acc
            ops.tensor_tensor(acc, base, part[:].rearrange(flat), ALU.add).then_inc(x2_sum, 1)

        @block.sync
        def _(sp):
            def at(v):
                return v if isinstance(v, int) else sp.snap(v)

            def load_x(n):
                t, taken = at(n % BLOCKS * BLOCK), at(n)
                if not isinstance(n, int) or n > 0:
                    sp.wait_ge(xT_ps, taken)
                for j in range(XTILES):
                    half = B // XTILES
                    sp.dma_start(x_rows[:, j, :], x[half * j:half * (j + 1), bass.ds(t, BLOCK), :]
                                 ).then_inc(x_in, 16)

            sp.dma_start(wh[:], L0_Wh.rearrange("(k p) n -> p k n", p=P)).then_inc(wh_in, 16)
            load_x(0)
            for name, src in (("eb1", eb1.rearrange("e (j p) -> (e j) p", p=P)),
                              ("sb1", sb1.rearrange("(j p) -> j p", p=P)),
                              ("eb2", eb2.rearrange("e (j p) -> (e j) p", p=P)),
                              ("sb2", sb2.rearrange("(j p) -> j p", p=P)),
                              ("L0_b", L0_b.rearrange("(j p) -> j p", p=P)),
                              ("L3_b", L3_b.rearrange("(j p) -> j p", p=P)),
                              ("L1_b", L1_b.rearrange("(j p) -> j p", p=P)),
                              ("cond", cond_1024.rearrange("b (j p) -> (b j) p", p=P))):
                sp.dma_start(rows[ROWS[name]:ROWS[name] + src.shape[0], :], src).then_inc(rows_in, 16)
            sp.dma_start(wx[:], L0_Wx.rearrange("(k p) n -> p k n", p=P)).then_inc(wx_in, 16)
            sp.dma_start(wh1[:], L1_Wh.rearrange("(k p) n -> p k n", p=P)).then_inc(w1_in, 16)
            sp.dma_start(wx1[:], L1_Wx.rearrange("(k p) n -> p k n", p=P)).then_inc(w1_in, 16)
            load_x(1)
            for e in range(NE):
                w1 = ew1[e] if e < E else sw1
                w2 = ew2[e] if e < E else sw2
                sp.dma_start(up_w[:, e], w1.rearrange("(k p) n -> p k n", p=P)).then_inc(expert_dma[e], 16)
                sp.dma_start(down_w[:, e], w2.rearrange("(j p) n -> p j n", p=P)).then_inc(expert_dma[e], 16)
            sp.dma_start(gate_w_sb[:], gate_w.rearrange("(k p) n -> p k n", p=P)).then_inc(gate_params_in, 16)
            sp.dma_start(time_w_sb[:], time_w.rearrange("(k p) n -> p k n", p=P)).then_inc(gate_params_in, 16)
            sp.dma_start(gate_b_sb[:], gate_b.rearrange("(a n) -> a n", a=1)).then_inc(gate_params_in, 16)
            sp.dma_start(time_b_sb[:], time_b.rearrange("(a n) -> a n", a=1)).then_inc(gate_params_in, 16)
            sp.wait_ge(wh_split, 1)
            sp.wait_ge(h0_z, 1)
            sp.dma_start(wh[:], L3_Wh.rearrange("(k p) n -> p k n", p=P)).then_inc(wh_in, 16)

            def store_experts(win, w, c):
                for e in range(NE):
                    if w == win.out[e]:
                        c_at = at(c)
                        if e == E:
                            written, count = y_shared, at(c + 1)
                        elif e in (1, 2):
                            written, count = y_masked, at(2 * c + e)
                        else:
                            written, count = y_evac, at(2 * (NE * c + e + 1))
                        sp.wait_ge(written, count)
                        dst = y_dram[bass.ds(c_at, 1), 1 + e].rearrange("a p n -> (a p) n")
                        sp.dma_start(dst, y[:, e].rearrange("p t h b -> p (t h b)")).then_inc(expert_dma[e], 16)

            def body_a(i):
                for s in range(PASS if lstm_at(i) else RNN_LAG):
                    if lstm_at(i) and s % BLOCK == 0 and not (isinstance(i, int) and i == s == 0):
                        load_x(2 * i + s // BLOCK + 1)
                    if experts_a(i, s) is not None:
                        store_experts(*experts_a(i, s))

            body_a(0)
            with sp.Fori(1, PASSES) as i:
                body_a(i)
            sp.wait_ge(xz_ps, FILLS * (BLOCKS + 1))
            sp.dma_start(wx[:], L3_Wx.rearrange("(k p) n -> p k n", p=P)).then_inc(wx_in, 16)
            body_a(PASSES)

            def load_block(n):
                if n > 0:
                    sp.wait_ge(x2_sum, E * n)
                for e in range(NE):
                    sp.wait_ge(expert_dma[e], 32 + 16 * (n + 1))
                for e in range(NE):
                    sp.dma_start(y_back[e].rearrange("p t h b -> p (t h b)"), y_dram[n, 1 + e]).then_inc(y_loaded, 16)

            def store(n):
                t = n * BLOCK
                sp.wait_ge(out_ready, n + 1)
                half = B // XTILES
                for j in range(XTILES):
                    sp.dma_start(out[half * j:half * (j + 1), t:t + BLOCK, :],
                                 out_rows[:, j, :]).then_inc(stored, 16)

            sp.wait_ge(wh_split, 2)
            load_block(0)
            load_block(1)
            for s in range(T):
                n, slot = divmod(s, BLOCK)
                if slot == 6 and n > 0:
                    store(n - 1)
                if slot == LOAD_SLOT and n + 2 < BLOCKS:
                    load_block(n + 2)
                if experts_b(s) is not None:
                    store_experts(*experts_b(s))
            store(BLOCKS - 1)
            sp.wait_ge(stored, 16 * XTILES * BLOCKS)
            for e in range(NE):
                sp.wait_ge(expert_dma[e], 32 + 16 * BLOCKS)

        @block.tensor
        def _(pe):
            def mm(out_ap, lhsT, rhs, start, stop):
                return nc.tensor.matmul(out_ap, lhsT, rhs, start=start, stop=stop, skip_group_check=True)

            def tb(ap):
                return ap.rearrange("p (t b) -> p t b", b=B)

            def gate_column(gate, m):
                return GATE_COLUMN[gate] * D + m * P

            def transposes(n):
                pe.wait_ge(x_in, 16 * XTILES * (n + 1))
                for k in range(HALVES):
                    for j in range(XTILES):
                        last = nc.tensor.transpose(bulk[0][:, (XTILES * k + j) * P:(XTILES * k + j + 1) * P],
                                                   x_rows[:, j, k * P:(k + 1) * P], ident[:])
                last.then_inc(xT_ps, 1)

            def x_product(fill, r, rhs):
                j, k = r // HALVES, r % HALVES
                m, gate = fill // 2, 2 * (fill % 2) + j
                c = gate_column(gate, m)
                last = mm(tb(bulk[fill % 2][:, j * TOK:(j + 1) * TOK]), wx[:, k, c:c + P], rhs[:, :, k, :],
                          k == 0, k == HALVES - 1)
                if r == 2 * HALVES - 1:
                    last.then_inc(xz_ps, 1)

            def lay_xz(parity, slot, lstm, steps):
                if not (isinstance(steps, int) and steps == 0):
                    pe.wait_ge(zs_ready, HALVES * steps)
                for m in range(HALVES):
                    out_z = z_banks[m][:].rearrange("p (n a b) -> p n a b", a=PARTS, b=B)[:, :, 0]
                    mm(out_z, ident_z[:, lstm], xz[:, parity, m, slot:slot + LAID].rearrange("p t g b -> p (t g) b"),
                       True, False)

            def lstm_step(step, starts, slot):
                for k in range(HALVES):
                    pe.wait_ge(h_ready, HALVES * (step + starts - 1) + k + 1)
                    for m in range(HALVES):
                        zp = z_of(slot, m).rearrange("p g a b -> p g (a b)")
                        for gate in range(GATES):
                            c = gate_column(gate, m)
                            for a in range(PARTS):
                                last = mm(zp[:, gate], wh16[:, a, k, c:c + P], h16[:, k].rearrange("p a b -> p (a b)"),
                                          False, k == a == 1)
                        if k == 1:
                            last.then_inc(z_ready, 1)

            def first_h(bank, n):
                c = gate_column(n % GATES, n // GATES)
                for k in range(HALVES):
                    last = mm(bank[:, n * B:(n + 1) * B], wh[:, k, c:c + P], cond_T()[:, k], k == 0, k == 1)
                if n == GATES * HALVES - 1:
                    last.then_inc(h0_z, 1)

            def rnn_products(parity, c):
                pe.wait_ge(rnn_x_ready, c + 1)
                for m in range(HALVES):
                    for k in range(HALVES):
                        last = mm(tb(bulk[1][:, m * TOK:(m + 1) * TOK]), wx1[:, k, m * P:(m + 1) * P],
                                  rnn_x[:, parity, :, k, :], k == 0, k == 1)
                last.then_inc(rnn_xz_ps, 1)

            def rnn_step(slot, parity, done, c):
                pe.wait_ge(rnn_h_ready, done + 1)
                for k in range(HALVES):
                    for m in range(HALVES):
                        for a in range(PARTS):
                            last = mm(z1[:, m * PARTS * B:(m + 1) * PARTS * B], wh1_16[:, a, k, m * P:(m + 1) * P],
                                      rnn_h16[:, k].rearrange("p a b -> p (a b)"), k == m == a == 0, k == a == 1)
                last.then_inc(rnn_z_ready, 1)

            def expert_products(win, w, c):
                for n in win.matmuls(w):
                    kind, q = items[n // MM_PER_ITEM]
                    r = n % MM_PER_ITEM
                    e, g = q // GPE, q % GPE
                    if kind == "up":
                        if r == 0 and q == 0:
                            pe.wait_ge(x1_ready, c + 1)
                        if r == 0 and q >= 2:
                            pe.wait_ge(u_ready, GROUPS * c + q - 1)
                        j, k = r // HALVES, r % HALVES
                        last = mm(tb(up_ps[q % 2][:, j * TOK:(j + 1) * TOK]),
                                  up_w[:, e, k, (GROUP * g + j) * P:(GROUP * g + j + 1) * P],
                                  x1[:, bass.ds(c * BLOCK, BLOCK), k, :], k == 0, k == 1)
                        if r == MM_PER_ITEM - 1:
                            last.then_inc(up_done, 1)
                    else:
                        if r == 0:
                            pe.wait_ge(hid_ready, GROUPS * c + q + 1)
                            if g == 0 and e > 0:
                                pe.wait_ge(y_evac, 2 * (NE * c + e))
                        m, j = r // GROUP, r % GROUP
                        last = mm(down_ps[:, m * TOK:(m + 1) * TOK],
                                  down_w[:, e, GROUP * g + j, m * P:(m + 1) * P],
                                  hid[:, q % 4, j * TOK:(j + 1) * TOK], g == 0 and r == 0,
                                  g == GPE - 1 and j == GROUP - 1)
                        if r == MM_PER_ITEM - 1 and g == GPE - 1:
                            last.then_inc(down_done, 1)

            pe.wait_ge(rows_in, 16 * 8)
            pe.wait_ge(consts, 2)
            nc.tensor.transpose(up_ps[0][:, 0:NROWS], rows[0:NROWS, :], ident[0:NROWS, 0:NROWS]).then_inc(vec_ps, 1)
            transposes(0)
            pe.wait_ge(wx_in, 16)
            pe.wait_ge(xT_ready, 1)
            for fill in range(FILLS):
                if fill >= 2:
                    pe.wait_ge(xz_ready, fill - 1)
                for r in range(2 * HALVES):
                    x_product(fill, r, xT[:, 0])
            pe.wait_ge(vec_ready, 1)
            pe.wait_ge(wh_in, 16)
            for n in range(GATES * HALVES):
                first_h(down_ps, n)
            pe.wait_ge(wh_split, 1)
            pe.wait_ge(h0_added, 1)
            lay_xz(0, 0, 0, 0)

            def rnn_first_h():
                pe.wait_ge(w1_in, 32)
                for m in range(HALVES):
                    for k in range(HALVES):
                        last = mm(z1[:, m * B:(m + 1) * B], wh1[:, k, m * P:(m + 1) * P], cond_T()[:, k],
                                  k == 0, k == 1)
                last.then_inc(rnn_z_ready, 1)

            def next_products(n, slot, rhs, with_rnn):
                if x_product_at(slot) is not None:
                    fill, r = x_product_at(slot)
                    if r == 0:
                        if fill == 1 and with_rnn is not None:
                            pe.wait_ge(rnn_xz_ready, with_rnn + 1)
                        if fill >= 2:
                            pe.wait_ge(xz_ready, FILLS * n + fill - 1)
                    x_product(fill, r, rhs)

            def body_a(i):
                for s in range(PASS if lstm_at(i) else RNN_LAG):
                    slot, parity = s % BLOCK, s // BLOCK
                    if lstm_at(i):
                        lstm_step(PASS * i + s, 1, slot)
                    if isinstance(i, int) and i == 0 and s == RNN_START:
                        rnn_first_h()
                    if isinstance(i, int) and i == 0 and s == RNN_LAG:
                        pe.wait_ge(first_rnn_ready, 1)
                        pe.wait_ge(wh1_split, 1)
                    if isinstance(i, int) and i == 0 and 0 <= s - FIRST_H3 < GATES * HALVES:
                        if s == FIRST_H3:
                            pe.wait_ge(wh_in, 32)
                        first_h(up_ps[0], s - FIRST_H3)
                    if slot == 0 and (lstm_at(i) or s == 0):
                        pe.wait_ge(xz_ready, FILLS * (2 * i + parity + 1))
                    r = rnn_at(i, s)
                    if r is not None:
                        rnn_step(*r)
                    if rnn_products_at(i, s) is not None:
                        rnn_products(*rnn_products_at(i, s))
                    if lstm_at(i):
                        n = 2 * i + parity + 1
                        if slot == 2:
                            transposes(n)
                        if slot == PRODUCTS_SLOT:
                            pe.wait_ge(xT_ready, n + 1)
                        next_products(n, slot, xT[:, 1 - parity], None if r is None else r[3])
                    if experts_a(i, s) is not None:
                        expert_products(*experts_a(i, s))
                    if lstm_at(i):
                        if slot == BLOCK - 1:
                            pe.wait_ge(xz_ready, FILLS * (n + 1))
                            lay_xz(1 - parity, 0, 0, PASS * i + s + 1)
                        elif slot % LAID == LAID - 1:
                            lay_xz(parity, slot + 1, 0, PASS * i + s + 1)

            body_a(0)
            for e in range(NE):
                pe.wait_ge(expert_dma[e], 32)
            pe.wait_ge(h0_added, 2)
            with pe.Fori(1, PASSES) as i:
                body_a(i)
            body_a(PASSES)

            pe.wait_ge(gate_params_in, 64)
            pe.wait_ge(rnn_xz_ready, BLOCKS)
            pe.wait_ge(g_dve, 1)
            for n in range(3 * HALVES):
                mm(bulk[0][0:B, 0:E], gate_in[:, n // HALVES, n % HALVES, :], gate_w_sb[:, n, :], n == 0, False)
            mm(bulk[0][0:B, 0:E], ones[0:1, 0:B], gate_b_sb[0:1, :], False, True)
            for n in range(HALVES):
                mm(bulk[1][0:B, 0:2 * E], silu[:, n * B:(n + 1) * B], time_w_sb[:, n, :], n == 0, False)
            mm(bulk[1][0:B, 0:2 * E], ones[0:1, 0:B], time_b_sb[0:1, :], False, True).then_inc(g_pe, 1)
            pe.wait_ge(g_dve, 2)
            mm(bulk[0][:, 0:E * B], ones[0:B, :], spread[:].rearrange("p e b -> p (e b)"), True, True).then_inc(g_pe, 1)

            XB = BLOCKS + 1
            pe.wait_ge(wx_in, 32)
            pe.wait_ge(x2_sum, E)
            for fill in range(FILLS):
                if fill >= 2:
                    pe.wait_ge(xz_ready, FILLS * XB + fill - 1)
                for r in range(2 * HALVES):
                    x_product(fill, r, x2[:, 0])
            pe.wait_ge(wh_split, 2)
            pe.wait_ge(h0_added, 3)
            lay_xz(0, 0, 1, T)

            def out_transposes(n):
                pe.wait_ge(x3_ready, n + 1)
                for j in range(XTILES):
                    for k in range(HALVES):
                        half = B // XTILES
                        last = nc.tensor.transpose(
                            bulk[0][:, j * D + k * P:j * D + (k + 1) * P],
                            x3[:, k, half * j:half * (j + 1)].rearrange("p b t -> p (b t)"), ident[:])
                last.then_inc(out_ps, 1)

            for s in range(T):
                n, slot = divmod(s, BLOCK)
                parity, last_block = n % 2, n == BLOCKS - 1
                lstm_step(T + s, 2, slot)
                if slot == 0:
                    pe.wait_ge(xz_ready, FILLS * (XB + n + 1))
                if slot == 1 and n > 0:
                    out_transposes(n - 1)
                if not last_block:
                    if slot == PRODUCTS_SLOT:
                        pe.wait_ge(x2_sum, E * (n + 2))
                        if n > 0:
                            pe.wait_ge(out_ready, n)
                    next_products(XB + n + 1, slot, x2[:, 1 - parity], None)
                if experts_b(s) is not None:
                    expert_products(*experts_b(s))
                if slot % LAID == LAID - 1 and slot < BLOCK - 1:
                    lay_xz(parity, slot + 1, 1, T + s + 1)
                elif slot == BLOCK - 1 and not last_block:
                    pe.wait_ge(xz_ready, FILLS * (XB + n + 2))
                    lay_xz(1 - parity, 0, 1, T + s + 1)
            out_transposes(BLOCKS - 1)

        @block.scalar
        def _(act):
            def lstm_gates(step, n):
                for m in range(HALVES):
                    act.wait_ge(zs_ready, HALVES * step + m + 1)
                    nc.scalar.activation(cell[:, m, 1:1 + GATES].rearrange("p g b -> p (g b)"),
                                         zs[:, m].rearrange("p g b -> p (g b)"), ACT.Tanh,
                                         scale=unscale[:, n:n + 1]).then_inc(gates_ready, 1)

            def lstm_cell(step):
                for m in range(HALVES):
                    act.wait_ge(cell_ready, HALVES * step + m + 1)
                    nc.scalar.activation(tanh_c[:, m], cell[:, m, 0], ACT.Tanh, scale=0.5).then_inc(cell_tanh, 1)

            def rnn_step(slot, parity, done, c):
                if slot == BLOCK // 2 and not (isinstance(c, int) and c == 0):
                    act.wait_ge(x1_ready, c)
                act.wait_ge(rnn_zs_ready, done + 1)
                nc.scalar.activation(rnn_h[:, parity, slot], rnn_zs[:], ACT.Tanh).then_inc(rnn_tanh, 1)

            def expert_steps(win, w, c):
                for q in range(GROUPS):
                    if w == win.tanh[q]:
                        act.wait_ge(poly_done, GROUPS * c + q + 1)
                        nc.scalar.activation(inner[:, q % 2], inner[:, q % 2], ACT.Tanh,
                                             scale=TANH_SCALE).then_inc(th_done, 1)
                def squares():
                    for q in range(GROUPS):
                        if w == win.square[q]:
                            act.wait_ge(u_ready, GROUPS * c + q + 1)
                            if q >= 2:
                                act.wait_ge(hid_ready, GROUPS * c + q - 1)
                            nc.scalar.activation(inner[:, q % 2], u[:, q % 4], ACT.Square,
                                                 scale=CUBIC ** 0.5).then_inc(sq_ready, 1)

                if win.square != win.up:
                    squares()
                for e in range(NE):
                    if w == win.out[e]:
                        act.wait_ge(down_done, NE * c + e + 1)
                        act.wait_ge(expert_dma[e], 32 + 16 * c)
                        for m in range(HALVES):
                            bias = column("eb2", HALVES * e + m) if e < E else column("sb2", m)
                            nc.scalar.activation(y[:, e, :, m, :],
                                                 down_ps[:, m * TOK:(m + 1) * TOK].rearrange("p (t b) -> p t b", b=B),
                                                 ACT.Identity, bias=bias, scale=0.5).then_inc(y_evac, 1)
                for q in range(GROUPS):
                    if w == win.up[q]:
                        act.wait_ge(up_done, GROUPS * c + q + 1)
                        if q >= 4:
                            act.wait_ge(hid_ready, GROUPS * c + q - 3)
                        e, g = q // GPE, q % GPE
                        for j in range(GROUP):
                            bias = column("eb1", e * TILES + g * GROUP + j) if e < E else column("sb1", g * GROUP + j)
                            last = nc.scalar.activation(u[:, q % 4, j * TOK:(j + 1) * TOK],
                                                        up_ps[q % 2][:, j * TOK:(j + 1) * TOK], ACT.Identity, bias=bias)
                        last.then_inc(u_ready, 1)
                if win.square == win.up:
                    squares()

            act.wait_ge(vec_ready, 1)
            nc.scalar.activation(silu[:], columns("cond", COLS), ACT.Sigmoid).then_inc(g_act, 1)

            def take_rnn_xz(c):
                act.wait_ge(rnn_xz_ps, c + 1)
                if not (isinstance(c, int) and c == 0):
                    act.wait_ge(rnn_zt_ready, BLOCK * c)
                for m in range(HALVES):
                    last = nc.scalar.activation(
                        rnn_xz[:, :, m, :], bulk[1][:, m * TOK:(m + 1) * TOK].rearrange("p (t b) -> p t b", b=B),
                        ACT.Identity, bias=column("L1_b", m))
                last.then_inc(rnn_xz_ready, 1)

            def body_a(i):
                for s in range(PASS if lstm_at(i) else RNN_LAG):
                    if lstm_at(i):
                        lstm_gates(PASS * i + s, 0)
                    r = rnn_at(i, s)
                    if r is not None:
                        rnn_step(*r)
                    if lstm_at(i):
                        lstm_cell(PASS * i + s)
                    if experts_a(i, s) is not None:
                        expert_steps(*experts_a(i, s))
                    if rnn_products_at(i, s) is not None:
                        take_rnn_xz(rnn_products_at(i, s)[1])

            body_a(0)
            with act.Fori(1, PASSES) as i:
                body_a(i)
            body_a(PASSES)

            act.wait_ge(g_shifted, 1)
            nc.scalar.activation(gs[:, 12:16], gs[:, 8:12], ACT.Exp).then_inc(g_act, 1)

            def take_out(n):
                act.wait_ge(out_ps, n + 1)
                if n > 0:
                    act.wait_ge(stored, 16 * XTILES * n)
                nc.scalar.copy(out_rows[:].rearrange("p j d -> p (j d)"), bulk[0][:]).then_inc(out_ready, 1)

            for s in range(T):
                lstm_gates(T + s, 2)
                lstm_cell(T + s)
                if s % BLOCK == 2 and s > BLOCK:
                    take_out(s // BLOCK - 1)
                if experts_b(s) is not None:
                    expert_steps(*experts_b(s))
            take_out(BLOCKS - 1)

        @block.vector
        def _(dve):
            chained = [0]

            def then(ins):
                chained[0] += 1
                ins.then_inc(g_chain, 1)
                dve.wait_ge(g_chain, chained[0])

            def find_max(n, w):
                nc.vector.tensor_reduce(w_max[:, n:n + 1], w[:].rearrange("p k n -> p (k n)"), AX_X, ALU.max,
                                        apply_absolute_value=True).then_inc(w_max_ready, 1)

            def find_scale(n):
                one = slice(n, n + 1)
                dve.wait_ge(w_top_ready, n + 1)
                then(nc.vector.tensor_scalar(w_pow[:, one], w_top[:, one], W_LEAST, None, ALU.max))
                then(nc.vector.tensor_scalar(w_pow[:, one].bitcast(I32), w_pow[:, one].bitcast(I32), 0x7F800000, None,
                                             ALU.bitwise_and))
                then(nc.vector.reciprocal(w_inv[:, one], w_pow[:, one]))
                then(nc.vector.tensor_scalar(up_scale[:, one], w_inv[:, one], W_TOP, None, ALU.mult))
                then(nc.vector.tensor_scalar(up_half[:, one], up_scale[:, one], 0.5, None, ALU.mult))
                then(nc.vector.tensor_scalar(z_scale[:, one], up_scale[:, one], H_SCALE, None, ALU.mult))
                nc.vector.tensor_scalar(unscale[:, one], w_pow[:, one], 1.0 / (W_TOP * H_SCALE), None, ALU.mult)
                if n != 1:
                    nc.vector.tensor_scalar(ident_z[:, n // 2], ident[:], z_scale[:, one], None, ALU.mult)

            def weight_parts(n):
                if n == 1:
                    return ((up_scale, slice(0, D)),)
                g_at = CANDIDATE * D
                return ((up_half, slice(0, g_at)), (up_scale, slice(g_at, g_at + D)))

            def split_high(n, w, w16):
                one = slice(n, n + 1)
                for factor, cols in weight_parts(n):
                    last = nc.vector.tensor_scalar(w16[:, 0, :, cols], w[:, :, cols], factor[:, one], None, ALU.mult)
                return last

            def split_low(n, w, w16, done):
                one = slice(n, n + 1)
                for factor, cols in weight_parts(n):
                    last = nc.vector.scalar_tensor_tensor(w16[:, 1, :, cols], w[:, :, cols], factor[:, one],
                                                          w16[:, 0, :, cols], ALU.mult, ALU.subtract)
                last.then_inc(done, 1)

            def split_weights(n, w, w16, done):
                find_scale(n)
                then(split_high(n, w, w16))
                split_low(n, w, w16, done)

            def start_lstm():
                nc.vector.memset(cell[:, :, 0], 0.0)
                nc.vector.memset(h16[:], 0.0).then_inc(h_ready, HALVES)

            def add_first_h(product):
                first = xz[:, 0, :, 0]
                product = product.rearrange("p (h g b) -> p h g b", h=HALVES, g=GATES)
                nc.vector.tensor_tensor(first[:, :, 0], first[:, :, 0], product[:, :, 0], ALU.add)
                nc.vector.scalar_tensor_tensor(
                    first[:, :, 1:GATES].rearrange("p h g b -> p h (g b)"),
                    product[:, :, 1:GATES].rearrange("p h g b -> p h (g b)"), 0.5,
                    first[:, :, 1:GATES].rearrange("p h g b -> p h (g b)"), ALU.mult, ALU.add).then_inc(h0_added, 1)

            def z_sum(step, slot, m):
                dve.wait_ge(z_ready, HALVES * step + m + 1)
                nc.vector.reduce_sum(zs[:, m], z_of(slot, m).rearrange("p g a b -> p g b a"),
                                     AX_X).then_inc(zs_ready, 1)

            def gate_products(step, m):
                dve.wait_ge(gates_ready, HALVES * step + m + 1)
                nc.vector.scalar_tensor_tensor(prod[:, m], cell[:, m, 2:4], 1.0, cell[:, m, 0:2], ALU.add,
                                               ALU.mult).then_inc(prod_ready, 1)

            def new_cell(step, m):
                dve.wait_ge(prod_ready, HALVES * step + m + 1)
                nc.vector.scalar_tensor_tensor(cell[:, m, 0], prod[:, m, 0], 0.5, prod[:, m, 1], ALU.mult,
                                               ALU.add).then_inc(cell_ready, 1)

            def output_gate(m):
                nc.vector.tensor_scalar(o_scaled[:, m], cell[:, m, GATES], 1.0, H_SCALE / 2, ALU.add,
                                        ALU.mult).then_inc(o_ready, 1)

            def h_high(step, slot, m):
                dve.wait_ge(cell_tanh, HALVES * step + m + 1)
                dve.wait_ge(o_ready, HALVES * step + m + 1)
                nc.vector.tensor_tensor(h_seq[:, slot, m], o_scaled[:, m], tanh_c[:, m], ALU.mult).then_inc(h_parts, 1)
                nc.vector.tensor_tensor(h16[:, m, 0], o_scaled[:, m], tanh_c[:, m], ALU.mult).then_inc(h_parts, 1)

            def h_low(step, slot, m):
                dve.wait_ge(h_parts, PARTS * (HALVES * step + m + 1))
                nc.vector.tensor_tensor(h16[:, m, 1], h_seq[:, slot, m], h16[:, m, 0],
                                        ALU.subtract).then_inc(h_ready, 1)

            def lstm_step(step, slot, rnn):
                z_sum(step, slot, 0)
                z_sum(step, slot, 1)
                if rnn is not None:
                    rnn_z(*rnn)
                gate_products(step, 0)
                if rnn is not None:
                    rnn_sum(*rnn)
                new_cell(step, 0)
                gate_products(step, 1)
                output_gate(0)
                new_cell(step, 1)
                output_gate(1)
                h_high(step, slot, 0)
                if rnn is not None:
                    rnn_high(*rnn)
                h_low(step, slot, 0)
                h_high(step, slot, 1)
                if rnn is not None:
                    rnn_low(*rnn)
                h_low(step, slot, 1)

            def rnn_z(slot, parity, done, c):
                if slot == 0:
                    dve.wait_ge(rnn_xz_ready, c + 1)
                zp = z1[:, 0:COLS * PARTS].rearrange("p (n a b) -> p n a b", a=PARTS, b=B)
                dve.wait_ge(rnn_z_ready, done + 2)
                nc.vector.scalar_tensor_tensor(rnn_zt[:], zp[:, :, 1], unscale[:, 1:2], rnn_xz[:, slot], ALU.mult,
                                               ALU.add).then_inc(rnn_zt_ready, 1)

            def rnn_sum(slot, parity, done, c):
                zp = z1[:, 0:COLS * PARTS].rearrange("p (n a b) -> p n a b", a=PARTS, b=B)
                dve.wait_ge(rnn_zt_ready, done + 1)
                nc.vector.scalar_tensor_tensor(rnn_zs[:], zp[:, :, 0], unscale[:, 1:2], rnn_zt[:], ALU.mult,
                                               ALU.add).then_inc(rnn_zs_ready, 1)

            def rnn_high(slot, parity, done, c):
                dve.wait_ge(rnn_tanh, done + 1)
                nc.vector.tensor_scalar(rnn_h16[:, :, 0], rnn_h[:, parity, slot], H_SCALE, None,
                                        ALU.mult).then_inc(rnn_h1_ready, 1)

            def rnn_low(slot, parity, done, c):
                dve.wait_ge(rnn_h1_ready, done + 1)
                nc.vector.scalar_tensor_tensor(rnn_h16[:, :, 1], rnn_h[:, parity, slot], H_SCALE, rnn_h16[:, :, 0],
                                               ALU.mult, ALU.subtract).then_inc(rnn_h_ready, 1)

            def take_xT(n, parity):
                dve.wait_ge(xT_ps, n + 1)
                for k in range(HALVES):
                    last = nc.vector.tensor_copy(
                        xT[:, parity, :, k, :].rearrange("p t b -> p b t"),
                        bulk[0][:, k * TOK:(k + 1) * TOK].rearrange("p (b t) -> p b t", t=BLOCK))
                last.then_inc(xT_ready, 1)

            def take_xz(n, fill, parity, bias, gates=(0, 1)):
                m, gate = fill // 2, 2 * (fill % 2)
                if 0 in gates:
                    dve.wait_ge(xz_ps, FILLS * n + fill + 1)
                for j in gates:
                    half = (None, ALU.add) if gate + j == 0 else (0.5, ALU.add, ALU.mult)
                    last = nc.vector.tensor_scalar(
                        xz[:, parity, m, :, gate + j, :],
                        bulk[fill % 2][:, j * TOK:(j + 1) * TOK].rearrange("p (t b) -> p t b", b=B),
                        column(bias, HALVES * GATE_COLUMN[gate + j] + m), *half)
                if 1 in gates:
                    last.then_inc(xz_ready, 1)

            def next_products(n, slot, parity, bias):
                for gate in range(2):
                    fill, r = divmod(slot - PRODUCTS_SLOT - 4 - gate, 5)
                    if 0 <= fill < FILLS and r == 0:
                        take_xz(n, fill, parity, bias, (gate,))

            def expert_steps(win, w, c):
                for q in range(GROUPS):
                    if w == win.hid[q]:
                        dve.wait_ge(th_done, GROUPS * c + q + 1)
                        nc.vector.scalar_tensor_tensor(hid[:, q % 4], inner[:, q % 2], 1.0, u[:, q % 4],
                                                       ALU.add, ALU.mult).then_inc(hid_ready, 1)
            dve.wait_ge(wh_in, 16)
            find_max(0, wh)
            dve.wait_ge(vec_ps, 1)
            nc.vector.tensor_copy(vec[:, 0:NROWS], up_ps[0][:, 0:NROWS]).then_inc(vec_ready, 1)
            take_xT(0, 0)
            dve.wait_ge(vec_ready, 1)
            for fill in range(FILLS):
                take_xz(0, fill, 0, "L0_b")
            split_weights(0, wh, wh16, wh_split)
            dve.wait_ge(h0_z, 1)
            dve.wait_ge(xz_ready, FILLS)
            add_first_h(down_ps[:, 0:GATES * COLS])
            start_lstm()
            def start_rnn(s):
                if s == RNN_START:
                    dve.wait_ge(w1_in, 32)
                    find_max(1, wh1)
                elif s == RNN_START + 1:
                    find_scale(1)
                elif s == RNN_START + 2:
                    then(split_high(1, wh1, wh1_16))
                    split_low(1, wh1, wh1_16, wh1_split)
                elif s == RNN_START + 3:
                    dve.wait_ge(rnn_z_ready, 1)
                    nc.vector.tensor_copy(first_rnn[:], z1[:, 0:COLS]).then_inc(first_rnn_ready, 1)
                    nc.vector.memset(rnn_h16[:], 0.0).then_inc(rnn_h_ready, 1)

            def sum_span(n):
                a, b_ = SPANS[n]
                return nc.vector.reduce_sum(sums[:, n].rearrange("p h b -> p (h b)"),
                                            x1[:, a:b_].rearrange("p t h b -> p (h b) t"), AX_X)

            def in_drain(s):
                if s == 1:
                    find_scale(2)
                elif s == 4:
                    split_high(2, wh, wh16).then_inc(high_ready, 1)
                elif s == 7:
                    dve.wait_ge(high_ready, 1)
                    split_low(2, wh, wh16, wh_split)
                elif s in (10, 13):
                    assert SPANS[1][1] <= T - BLOCK
                    dve.wait_ge(x1_ready, BLOCKS - 1)
                    sum_span((s - 10) // 3)

            def body_a(i):
                for s in range(PASS if lstm_at(i) else RNN_LAG):
                    slot, parity = s % BLOCK, s // BLOCK
                    step = PASS * i + s
                    r = rnn_at(i, s)
                    if lstm_at(i):
                        lstm_step(step, slot, r)
                    elif r is not None:
                        for part_ in (rnn_z, rnn_sum, rnn_high, rnn_low):
                            part_(*r)
                    if lstm_at(i):
                        n = 2 * i + parity + 1
                        if isinstance(i, int) and i == 0:
                            start_rnn(s)
                        if isinstance(i, int) and i == 0 and s == FIRST_H3 + GATES * HALVES:
                            dve.wait_ge(h0_z, 2)
                            nc.vector.tensor_copy(first_h3[:], up_ps[0][:, 0:GATES * COLS]).then_inc(h0_added, 1)
                            dve.wait_ge(wh_in, 32)
                            find_max(2, wh)
                        if slot == 3:
                            take_xT(n, 1 - parity)
                        next_products(n, slot, 1 - parity, "L0_b")
                        if slot == BLOCK - 1:
                            dve.wait_ge(h_parts, PARTS * HALVES * (step + 1))
                            flat = "p t h b -> p (t h b)"
                            nc.vector.scalar_tensor_tensor(rnn_x[:, parity].rearrange(flat), h_seq[:].rearrange(flat),
                                                           1 / H_SCALE, xT[:, parity].rearrange(flat), ALU.mult,
                                                           ALU.add).then_inc(rnn_x_ready, 1)
                    if experts_a(i, s) is not None:
                        expert_steps(*experts_a(i, s))
                    if isinstance(i, int) and i == 0 and s == BLOCK:
                        dve.wait_ge(rnn_xz_ready, 1)
                        then(nc.vector.tensor_tensor(rnn_xz[:, 0].rearrange("p h b -> p (h b)"),
                                                     rnn_xz[:, 0].rearrange("p h b -> p (h b)"), first_rnn[:],
                                                     ALU.add))
                    if not lstm_at(i):
                        in_drain(s)

            body_a(0)
            with dve.Fori(1, PASSES) as i:
                body_a(i)
            body_a(PASSES)

            dve.wait_ge(x1_ready, BLOCKS)
            then(sum_span(2))
            head, wrist, proprio = (sums[:, n] for n in range(3))
            lengths = [b_ - a for a, b_ in SPANS]
            then(nc.vector.tensor_tensor(gate_in[:, 1], head, proprio, ALU.add))
            then(nc.vector.tensor_tensor(gate_in[:, 2], wrist, proprio, ALU.add))
            then(nc.vector.tensor_tensor(gate_in[:, 0], gate_in[:, 1], wrist, ALU.add))
            then(nc.vector.tensor_scalar(gate_in[:, 0], gate_in[:, 0], 1.0 / T, None, ALU.mult))
            then(nc.vector.tensor_scalar(gate_in[:, 1], gate_in[:, 1], 1.0 / (lengths[0] + lengths[2]), None, ALU.mult))
            then(nc.vector.tensor_scalar(gate_in[:, 2], gate_in[:, 2], 1.0 / (lengths[1] + lengths[2]), None, ALU.mult))
            dve.wait_ge(g_act, 1)
            then(nc.vector.tensor_tensor(gtmp[:], silu[:], columns("cond", COLS), ALU.mult))
            nc.vector.tensor_copy(silu[:].rearrange("p (h b) -> p h b", h=HALVES),
                                  gtmp[:].rearrange("p (b h) -> p h b", h=HALVES)).then_inc(g_dve, 1)
            dve.wait_ge(g_pe, 1)
            mod, logits, shifted, expd = gs[:, 0:8], gs[:, 16:20], gs[:, 8:12], gs[:, 12:16]
            score, rank, top, wgt = gs[:, 20:24], gs[:, 24:28], gs[:, 28:32], gs[:, 32:36]
            one = gs[:, 40:41]
            then(nc.vector.tensor_copy(mod, bulk[1][0:B, 0:2 * E]))
            then(nc.vector.tensor_scalar(mod[:, 0:E], mod[:, 0:E], 1.0, None, ALU.add))
            then(nc.vector.tensor_tensor(logits, bulk[0][0:B, 0:E], mod[:, 0:E], ALU.mult))
            then(nc.vector.tensor_tensor(logits, logits, mod[:, E:2 * E], ALU.add))
            then(nc.vector.reduce_max(one, logits, AX_X))
            nc.vector.tensor_scalar(shifted, logits, one, None, ALU.subtract).then_inc(g_shifted, 1)
            dve.wait_ge(g_act, 2)
            then(nc.vector.reduce_sum(gs[:, 41:42], expd, AX_X))
            then(nc.vector.reciprocal(gs[:, 42:43], gs[:, 41:42]))
            then(nc.vector.tensor_scalar(score, expd, gs[:, 42:43], None, ALU.mult))
            then(nc.vector.memset(rank, 0.0))
            for j in range(E):
                s_j = score[:, j:j + 1]
                if j > 0:
                    then(nc.vector.scalar_tensor_tensor(rank[:, 0:j], score[:, 0:j], s_j, rank[:, 0:j],
                                                        ALU.is_lt, ALU.add))
                if j < E - 1:
                    then(nc.vector.scalar_tensor_tensor(rank[:, j + 1:E], score[:, j + 1:E], s_j, rank[:, j + 1:E],
                                                        ALU.is_le, ALU.add))
            then(nc.vector.scalar_tensor_tensor(top, rank, 2.0, score, ALU.is_lt, ALU.mult))
            then(nc.vector.reduce_sum(gs[:, 43:44], top, AX_X))
            then(nc.vector.tensor_scalar(gs[:, 44:45], gs[:, 43:44], 1e-8, None, ALU.add))
            then(nc.vector.reciprocal(gs[:, 45:46], gs[:, 44:45]))
            then(nc.vector.tensor_scalar(wgt, top, gs[:, 45:46], None, ALU.mult))
            nc.vector.tensor_tensor(spread[:], wgt[:, :, None].to_broadcast([B, E, B]),
                                    ident[0:B, None, 0:B].to_broadcast([B, E, B]), ALU.mult).then_inc(g_dve, 1)
            dve.wait_ge(g_pe, 2)
            nc.vector.tensor_copy(wb[:].rearrange("p e b -> p (e b)"), bulk[0][:, 0:E * B]).then_inc(wb_ready, 1)
            dve.wait_ge(wb_ready, 1)
            for k in range(1, NE):
                combine(nc.vector, dve, 0, 0, k)

            XB = BLOCKS + 1
            for fill in range(FILLS):
                take_xz(XB, fill, 0, "L3_b")
            dve.wait_ge(xz_ready, FILLS * (XB + 1))
            dve.wait_ge(h0_added, 2)
            add_first_h(first_h3[:])
            start_lstm()

            for s in range(T):
                n, slot = divmod(s, BLOCK)
                parity = n % 2
                lstm_step(T + s, slot, None)
                if n < BLOCKS - 1:
                    next_products(XB + n + 1, slot, 1 - parity, "L3_b")
                if slot == BLOCK - 1:
                    dve.wait_ge(h_parts, PARTS * HALVES * (T + s + 1))
                    for m in range(HALVES):
                        last = nc.vector.scalar_tensor_tensor(
                            x3[:, m], h_seq[:, :, m, :].rearrange("p t b -> p b t"), 1 / H_SCALE,
                            x2[:, parity, :, m, :].rearrange("p t b -> p b t"), ALU.mult, ALU.add)
                    last.then_inc(x3_ready, 1)
                if experts_b(s) is not None:
                    expert_steps(*experts_b(s))

        @block.gpsimd
        def _(pool):
            nc.gpsimd.memset(ident[:], 0.0).then_inc(pool_c, 1)
            nc.gpsimd.memset(ones[:], 1.0).then_inc(consts, 1)
            pool.wait_ge(pool_c, 1)
            nc.gpsimd.affine_select(out=ident[:], in_=ident[:], compare_op=ALU.not_equal, fill=1.0, base=0,
                                    pattern=[[-1, P]], channel_multiplier=1).then_inc(consts, 1)
            nc.gpsimd.memset(keep[:], 1.0).then_inc(pool_c, 1)
            pool.wait_ge(pool_c, 2)
            nc.gpsimd.memset(keep[:, 0, THIRD:2 * THIRD], 0.0).then_inc(pool_c, 1)
            nc.gpsimd.memset(keep[:, 1, 0:THIRD], 0.0).then_inc(pool_c, 1)
            pool.wait_ge(pool_c, 4)

            def spread_max(n):
                pool.wait_ge(w_max_ready, n + 1)
                nc.gpsimd.partition_all_reduce(w_top[:, n:n + 1], w_max[:, n:n + 1], P,
                                               bass.bass_isa.ReduceOp.max).then_inc(w_top_ready, 1)

            spread_max(0)
            spread_max(1)

            def expert_steps(win, w, c):
                for q in range(GROUPS):
                    if w == win.square[q]:
                        n = GROUPS * c + q
                        pool.wait_ge(sq_ready, n + 1)
                        v = inner[:, q % 2]
                        nc.gpsimd.tensor_tensor(v, v, u[:, q % 4], ALU.mult).then_inc(pool_chain, 1)
                        pool.wait_ge(pool_chain, n + 1)
                        nc.gpsimd.tensor_tensor(v, v, u[:, q % 4], ALU.add).then_inc(poly_done, 1)
                for e in (1, 2, E):
                    if w == win.out[e]:
                        pool.wait_ge(y_evac, 2 * (NE * c + e + 1))
                        if e < E:
                            mask = keep[:, e - 1, bass.ds(c * BLOCK, BLOCK)]
                            nc.gpsimd.tensor_tensor(
                                y[:, e].rearrange("p t h b -> p t (h b)"), y[:, e].rearrange("p t h b -> p t (h b)"),
                                mask[:, :, None].to_broadcast([P, BLOCK, COLS]), ALU.mult).then_inc(y_masked, 1)
                        else:
                            nc.gpsimd.tensor_tensor(
                                y[:, e].rearrange("p t h b -> p (t h b)"), y[:, e].rearrange("p t h b -> p (t h b)"),
                                x1[:, bass.ds(c * BLOCK, BLOCK)].rearrange("p t h b -> p (t h b)"),
                                ALU.add).then_inc(y_shared, 1)

            def body_a(i):
                for s in range(PASS if lstm_at(i) else RNN_LAG):
                    r = rnn_at(i, s)
                    if r is not None and r[0] == BLOCK - 1:
                        _, parity, done, c = r
                        pool.wait_ge(rnn_tanh, done + 1)
                        nc.gpsimd.tensor_tensor(x1[:, bass.ds(c * BLOCK, BLOCK)].rearrange("p t h b -> p (t h b)"),
                                                rnn_x[:, parity].rearrange("p t h b -> p (t h b)"),
                                                rnn_h[:, parity].rearrange("p t h b -> p (t h b)"),
                                                ALU.add).then_inc(x1_ready, 1)
                    if experts_a(i, s) is not None:
                        expert_steps(*experts_a(i, s))

            spread_max(2)
            body_a(0)
            with pool.Fori(1, PASSES) as i:
                body_a(i)
            body_a(PASSES)

            pool.wait_ge(wb_ready, 1)
            for s in range(T):
                n, slot = divmod(s, BLOCK)
                if slot in (1, 3, 5, 7) and n < BLOCKS - 1:
                    combine(nc.gpsimd, pool, n + 1, (n + 1) % 2, (slot + 1) // 2)
                if experts_b(s) is not None:
                    expert_steps(*experts_b(s))


_INS = ["x", "cond_1024", "L0_cond_Wx", "L0_cond_Wh", "L0_cond_b", "L1_cond_Wx", "L1_cond_Wh", "L1_cond_b",
        "L2_cond_gate_w", "L2_cond_gate_b", "L2_cond_time_w", "L2_cond_time_b", "L2_cond_ew1", "L2_cond_eb1",
        "L2_cond_ew2", "L2_cond_eb2", "L2_cond_sw1", "L2_cond_sb1", "L2_cond_sw2", "L2_cond_sb2",
        "L3_cond_Wx", "L3_cond_Wh", "L3_cond_b"]


def kernel(**inputs):
    import numpy as _np
    import concourse.bacc as _bacc
    from concourse import mybir as _mybir
    from concourse.bass_utils import run_bass_kernel_spmd as _run

    nc = _bacc.Bacc("TRN2", target_bir_lowering=False, num_devices=1)
    arrays, args = {}, []
    for name in _INS:
        a = _np.ascontiguousarray(inputs[name])
        arrays[f"in_{name}_dram"] = a
        args.append(nc.dram_tensor(f"in_{name}_dram", a.shape, _mybir.dt.from_np(a.dtype), kind="ExternalInput").ap())
    out = nc.dram_tensor("out_dram", (8, 256, 256), _mybir.dt.float32, kind="ExternalOutput").ap()
    cond_residual_kernel(nc, *args, out)
    r = _run(nc, [arrays], core_ids=[0])
    return r.results[0]["out_dram"]
```
